# Optimizing a Trainium2 kernel written in Bass

```python
import numpy as np
import jax
import jax.numpy as jnp

def _softmax(x, axis=-1):
    return jax.nn.softmax(x, axis=axis)

def _gelu(x):
    return jax.nn.gelu(x, approximate=True)

def _silu(x):
    return jax.nn.silu(x)

def _sigmoid(x):
    return jax.nn.sigmoid(x)

def _layernorm(x, axis=-1, eps=1e-05):
    m = jnp.mean(x, axis=axis, keepdims=True)
    v = jnp.var(x, axis=axis, keepdims=True)
    return (x - m) / jnp.sqrt(v + eps)

def _scatter_add(tgt, idx, src, axis=0):
    return tgt.at[idx].add(src)

def _segment_sum(src, seg, n):
    return jax.ops.segment_sum(src, seg, n)
kernel_name = 'mk_seq_postln_d1_jaxref_r4_cf2db9'

def setup_inputs(seed: int=0):
    np.random.seed(seed)
    _w = jnp.asarray

    def _L0_attn_setup():
        import jax, jax.numpy as jnp
        import numpy as np
        B, L, D, H = (4, 256, 256, 16)
        HD = D // H
        MAX_LEN = 256
        SCALE = HD ** 0.5

        def _rel_idx(seq_len):
            r = jnp.arange(seq_len)
            dist = r[None, :] - r[:, None]
            return jnp.clip(dist, -MAX_LEN, MAX_LEN) + MAX_LEN
        key = jax.random.key(seed)
        ks = jax.random.split(key, 7)
        sd = 1.0 / np.sqrt(D)
        x = jax.random.normal(ks[0], (B, L, D), dtype=jnp.float32)
        Wq = jax.random.normal(ks[1], (D, D), dtype=jnp.float32) * sd
        Wk = jax.random.normal(ks[2], (D, D), dtype=jnp.float32) * sd
        Wv = jax.random.normal(ks[3], (D, D), dtype=jnp.float32) * sd
        Wo = jax.random.normal(ks[4], (D, D), dtype=jnp.float32) * sd
        pek = jax.random.normal(ks[5], (2 * MAX_LEN + 1, HD), dtype=jnp.float32) / np.sqrt(HD)
        pev = jax.random.normal(ks[6], (2 * MAX_LEN + 1, HD), dtype=jnp.float32) / np.sqrt(HD)
        return {'x': x, 'Wq': Wq, 'Wk': Wk, 'Wv': Wv, 'Wo': Wo, 'pek': pek, 'pev': pev}
    _L0_attn_in = _L0_attn_setup()

    def _L0_ffn_setup():
        import jax, jax.numpy as jnp
        import numpy as np
        DIM = 256
        HIDDEN = 768
        SCALE = 1.0 / 127.0

        def _dequant(w_int, dtype):
            return w_int.astype(dtype) * jnp.asarray(SCALE, dtype)
        key = jax.random.key(seed)
        k_x, k_g, k_u, k_d = jax.random.split(key, 4)
        x = jax.random.normal(k_x, (4, 512, DIM), dtype=jnp.float32)
        w_gate = jax.random.randint(k_g, (HIDDEN, DIM), -127, 128, dtype=jnp.int32)
        w_up = jax.random.randint(k_u, (HIDDEN, DIM), -127, 128, dtype=jnp.int32)
        w_down = jax.random.randint(k_d, (DIM, HIDDEN), -127, 128, dtype=jnp.int32)
        return {'x': x, 'w_gate': w_gate, 'w_up': w_up, 'w_down': w_down}
    _L0_ffn_in = _L0_ffn_setup()
    _d = {'L0_attn_x': _L0_attn_in['x'], 'L0_attn_Wq': _L0_attn_in['Wq'], 'L0_attn_Wk': _L0_attn_in['Wk'], 'L0_attn_Wv': _L0_attn_in['Wv'], 'L0_attn_Wo': _L0_attn_in['Wo'], 'L0_attn_pek': _L0_attn_in['pek'], 'L0_attn_pev': _L0_attn_in['pev'], 'L0_ffn_w_gate': _L0_ffn_in['w_gate'], 'L0_ffn_w_up': _L0_ffn_in['w_up'], 'L0_ffn_w_down': _L0_ffn_in['w_down']}
    _x0 = _d['L0_attn_x']
    _d['L0_attn_x'] = jax.random.normal(jax.random.fold_in(jax.random.key(seed), 1), (16, 1024, 256), dtype=_x0.dtype)
    del _x0
    return _d

def reference(L0_attn_x, L0_attn_Wq, L0_attn_Wk, L0_attn_Wv, L0_attn_Wo, L0_attn_pek, L0_attn_pev, L0_ffn_w_gate, L0_ffn_w_up, L0_ffn_w_down):

    def _L0_attn_ref(x, Wq, Wk, Wv, Wo, pek, pev):
        import jax, jax.numpy as jnp
        import numpy as np
        B, L, D, H = (4, 256, 256, 16)
        HD = D // H
        MAX_LEN = 256
        SCALE = HD ** 0.5

        def _rel_idx(seq_len):
            r = jnp.arange(seq_len)
            dist = r[None, :] - r[:, None]
            return jnp.clip(dist, -MAX_LEN, MAX_LEN) + MAX_LEN
        b, s, _ = x.shape

        def proj(W):
            return (x @ W.T).reshape(b, s, H, HD).transpose(0, 2, 1, 3)
        Q, K, V = (proj(Wq), proj(Wk), proj(Wv))
        scores = jnp.einsum('bhqd,bhkd->bhqk', Q, K) / SCALE
        idx = _rel_idx(s)
        rel_k = pek[idx]
        scores = scores + jnp.einsum('bhqd,qkd->bhqk', Q, rel_k) / SCALE
        causal = jnp.tril(jnp.ones((s, s), dtype=bool))
        scores = jnp.where(causal[None, None], scores, -jnp.inf)
        attn = jax.nn.softmax(scores, axis=-1)
        out = jnp.einsum('bhqk,bhkd->bhqd', attn, V)
        rel_v = pev[idx]
        out = out + jnp.einsum('bhqk,qkd->bhqd', attn, rel_v)
        out = out.transpose(0, 2, 1, 3).reshape(b, s, D)
        return out @ Wo.T

    def _L0_ffn_ref(x, w_gate, w_up, w_down):
        import jax, jax.numpy as jnp
        import numpy as np
        DIM = 256
        HIDDEN = 768
        SCALE = 1.0 / 127.0

        def _dequant(w_int, dtype):
            return w_int.astype(dtype) * jnp.asarray(SCALE, dtype)
        wg = _dequant(w_gate, x.dtype)
        wu = _dequant(w_up, x.dtype)
        wd = _dequant(w_down, x.dtype)
        gate = jnp.einsum('bsd,hd->bsh', x, wg)
        up = jnp.einsum('bsd,hd->bsh', x, wu)
        h = jax.nn.silu(gate) * up
        return jnp.einsum('bsh,dh->bsd', h, wd)
    x = L0_attn_x
    x = _layernorm(x + _L0_attn_ref(x, L0_attn_Wq, L0_attn_Wk, L0_attn_Wv, L0_attn_Wo, L0_attn_pek, L0_attn_pev), axis=-1)
    x = _layernorm(x + _L0_ffn_ref(x, L0_ffn_w_gate, L0_ffn_w_up, L0_ffn_w_down), axis=-1)
    return x

_drawn_inputs = setup_inputs


def setup_inputs(seed=0):
    import zlib

    import numpy as np

    out = dict(_drawn_inputs(seed))
    spreads = {}
    factors = {}
    for name, (base, spread) in spreads.items():
        noise = np.random.default_rng([zlib.crc32(name.encode()), seed]).standard_normal(out[name].shape)
        drawn = base * np.exp(spread * noise) if base else spread * noise
        out[name] = jnp.asarray(drawn.astype(out[name].dtype))
    for name, factor in factors.items():
        out[name] = (out[name] * factor).astype(out[name].dtype)
    return out
```

```python
from contextlib import ExitStack

import concourse.bass as bass
from concourse import mybir

ALU = mybir.AluOpType
ACT = mybir.ActivationFunctionType
F32 = mybir.dt.float32
BF16 = mybir.dt.bfloat16
I32 = mybir.dt.int32
AX = mybir.AxisListType

P = 128
HD = 16
MAXD = 256
GRP = 4
CHUNK = 512
CT = CHUNK // P
TERMS_Q = (0, 0, 1, 1, 0, 2)
TERMS_K = (0, 1, 0, 1, 2, 0)
ROWS = HD * len(TERMS_Q)
NEG = -1.0e30
BIG = 3.0e38
EPS = 1e-5
W_SCALE = 1.0 / 127.0
PW = 2 * P + MAXD
BAND = MAXD + P
PPITCH = P * BAND + MAXD


def peeled(eng, n, body):
    body(0, True, n == 1)
    if n > 2:
        with eng.Fori(1, n - 1) as i:
            body(i, False, False)
    if n > 1:
        body(n - 1, False, True)


def project(nc, x, wq, wk, wv, pek, pev, qk_scr, v_scr):
    nb, seq, dim = x.shape
    n_iter = nb
    assert seq == 2 * CHUNK and dim == 2 * P
    with ExitStack() as ctx:
        sb = lambda n, s, d=F32: ctx.enter_context(nc.sbuf_tensor(n, s, d))
        ps = lambda n, s: ctx.enter_context(nc.psum_tensor(n, s, F32))
        sem = lambda n: ctx.enter_context(nc.semaphore(n))
        ident = sb("p_ident", [P, P])
        w_in = sb("p_w_in", [P, 3, 2, dim])
        w_t = sb("p_w_t", [P, 3, 2, dim])
        pe0 = sb("p_pe0", [P, 1])
        pv0 = sb("p_pv0", [P, HD])
        x_in = sb("p_x_in", [P, 2, CT, dim])
        x_t = sb("p_x_t", [P, 2, 2, CHUNK])
        full = sb("p_full", [P, 2, CHUNK])
        rest = sb("p_rest", [P, 2, CHUNK])
        parts = sb("p_parts", [P, 2, 3, CHUNK], BF16)
        v_out = sb("p_v_out", [P, 2, 2, dim // HD, 2 * HD])
        tr_ps = ps("p_tr_ps", [P, 2, CHUNK])
        pr_ps = ps("p_pr_ps", [P, 2, CHUNK])
        v_ps = ps("p_v_ps", [P, 2, 2, dim])
        id_zero, id_ready = sem("p_id_zero"), sem("p_id_ready")
        w_loaded, w_tr, w_ready = sem("p_w_loaded"), sem("p_w_tr"), sem("p_w_ready")
        v_pad = sem("p_v_pad")
        x_loaded = [sem(f"p_x_loaded{i}") for i in range(2)]
        xt_mm, xt_ready = sem("p_xt_mm"), sem("p_xt_ready")
        pr_mm, full_ready = sem("p_pr_mm"), sem("p_full_ready")
        hi_ready, rest_ready, mid_ready, lo_ready = sem("p_hi"), sem("p_rest_ready"), sem("p_mid"), sem("p_lo")
        v_mm, v_ready = sem("p_v_mm"), sem("p_v_ready")
        part_saved = [sem(f"p_part_saved{i}") for i in range(2)]
        v_saved = [sem(f"p_v_saved{i}") for i in range(2)]
        block = ctx.enter_context(nc.Block())

        @block.sync
        def _(sp):
            for i, w in enumerate((wq, wk, wv)):
                sp.dma_start(w_in[:, i], w.rearrange("(t p) d -> p t d", p=P)).then_inc(w_loaded, 16)
            for h in range(P // HD):
                sp.dma_start(pe0[h * HD:(h + 1) * HD, :], pek[0:1, :].rearrange("a d -> d a")).then_inc(w_loaded, 16)
            sp.dma_start(pv0[:, :], pev[0:1, :].to_broadcast([P, HD])).then_inc(w_loaded, 16)

            def load(r, j):
                sp.dma_start(x_in[:, j], x[r, j * CHUNK:(j + 1) * CHUNK, :]
                             .rearrange("(t p) d -> p t d", p=P)).then_inc(x_loaded[j], 16)

            load(0, 0)

            def body(r, first, last):
                for j in range(2):
                    if j == 0 or not last:
                        if j or not first:
                            sp.wait_ge(xt_mm, 2 * (2 * r + j))
                        load(r + j, 1 - j)
                    for m in range(4):
                        sp.wait_ge(lo_ready, 4 * (2 * r + j) + m + 1)
                        sp.dma_start(qk_scr[m // 2, r * 2 + m % 2, :, :, j * CHUNK:(j + 1) * CHUNK]
                                     .rearrange("s p t -> p s t"), parts[:, m % 2]).then_inc(part_saved[m % 2], 16)
                    for h in range(2):
                        sp.wait_ge(v_ready, 2 * (2 * r + j) + h + 1)
                        for g in range(4):
                            sp.dma_start(
                                v_scr[r * 4 + g, j * CHUNK + h * 2 * P:j * CHUNK + (h + 1) * 2 * P, :]
                                .rearrange("(t p) c -> p t c", p=P),
                                v_out[:, h, :, g * GRP:(g + 1) * GRP, :].rearrange("p t h c -> p t (h c)")) \
                                .then_inc(v_saved[h], 16)
            peeled(sp, n_iter, body)
            for i in range(2):
                sp.wait_ge(part_saved[i], 16 * 4 * n_iter)
                sp.wait_ge(v_saved[i], 16 * 8 * n_iter)

        @block.gpsimd
        def _(pool):
            pool.memset(ident[:, :], 0.0).then_inc(id_zero, 1)
            pool.wait_ge(id_zero, 1)
            pool.affine_select(out=ident[:, :], in_=ident[:, :], compare_op=ALU.not_equal, fill=1.0, base=0,
                               pattern=[[-1, P]], channel_multiplier=1).then_inc(id_ready, 1)
            pool.memset(v_out[:, :, :, :, :], 0.0).then_inc(v_pad, 1)

            def body(r, first, last):
                for j in range(2):
                    for m in range(4):
                        n = 4 * (2 * r + j) + m
                        pool.wait_ge(mid_ready, n + 1)
                        pool.tensor_tensor(parts[:, m % 2, 2], rest[:, m % 2], parts[:, m % 2, 1], ALU.subtract) \
                            .then_inc(lo_ready, 1)
            peeled(pool, n_iter, body)

        @block.tensor
        def _(pe):
            pe.wait_ge(id_ready, 1)
            pe.wait_ge(w_loaded, 16 * 12)
            for i in range(3):
                for c in range(2):
                    n = 2 * i + c
                    if n >= 2:
                        pe.wait_ge(w_ready, n - 1)
                    for t in range(2):
                        mm = pe.transpose(tr_ps[:, n % 2, t * P:(t + 1) * P], w_in[:, i, t, c * P:(c + 1) * P], ident[:, :])
                    mm.then_inc(w_tr, 1)
            pe.wait_ge(w_ready, 6)

            def transposes(r, j):
                pe.wait_ge(x_loaded[j], 16 * (r + 1))
                for c in range(2):
                    for t in range(CT):
                        mm = pe.transpose(tr_ps[:, c, t * P:(t + 1) * P], x_in[:, j, t, c * P:(c + 1) * P], ident[:, :])
                    mm.then_inc(xt_mm, 1)

            transposes(0, 0)

            def body(r, first, last):
                for j in range(2):
                    pe.wait_ge(xt_ready, 2 * (2 * r + j) + 2)
                    for m in range(4):
                        n = 4 * (2 * r + j) + m
                        if m >= 2 or j or not first:
                            pe.wait_ge(full_ready, n - 1)
                        for c in range(2):
                            mm = pe.matmul(pr_ps[:, m % 2], w_t[:, m // 2, c, (m % 2) * P:(m % 2 + 1) * P],
                                           x_t[:, j, c], start=(c == 0), stop=(c == 1))
                        mm.then_inc(pr_mm, 1)
                    if j == 0 or not last:
                        transposes(r + j, 1 - j)
                    for h in range(2):
                        if j or not first:
                            pe.wait_ge(v_ready, 2 * (2 * r + j) + h - 1)
                        for t in range(2):
                            for c in range(2):
                                mm = pe.matmul(v_ps[:, h, t], x_t[:, j, c, (2 * h + t) * P:(2 * h + t + 1) * P],
                                               w_t[:, 2, c], start=(t == 0 and c == 0), stop=(c == 1),
                                               skip_group_check=True)
                        mm.then_inc(v_mm, 1)
            peeled(pe, n_iter, body)

        @block.scalar
        def _(act):
            for n in range(6):
                act.wait_ge(w_tr, n + 1)
                act.activation(w_t[:, n // 2, n % 2], tr_ps[:, n % 2, 0:dim], ACT.Copy).then_inc(w_ready, 1)

            def take_x(r, j):
                for c in range(2):
                    act.wait_ge(xt_mm, 2 * (2 * r + j) + c + 1)
                    act.activation(x_t[:, j, c], tr_ps[:, c], ACT.Copy).then_inc(xt_ready, 1)

            take_x(0, 0)

            def body(r, first, last):
                for j in range(2):
                    def middle(m):
                        act.wait_ge(rest_ready, 4 * (2 * r + j) + m + 1)
                        if m >= 2 or j or not first:
                            act.wait_ge(part_saved[m % 2], 16 * (2 * (2 * r + j) + m // 2))
                        act.activation(parts[:, m % 2, 1], rest[:, m % 2], ACT.Copy).then_inc(mid_ready, 1)

                    for m in range(4):
                        n = 4 * (2 * r + j) + m
                        act.wait_ge(pr_mm, n + 1)
                        if m >= 2 or j or not first:
                            act.wait_ge(rest_ready, n - 1)
                        if m < 2:
                            act.activation(full[:, m % 2], pr_ps[:, m % 2], ACT.Copy, scale=float(HD) ** -0.5) \
                                .then_inc(full_ready, 1)
                        else:
                            act.activation(full[:, m % 2], pr_ps[:, m % 2], ACT.Identity, bias=pe0[:, 0:1]) \
                                .then_inc(full_ready, 1)
                        if m:
                            middle(m - 1)
                    if j == 0 or not last:
                        if j or not first:
                            act.wait_ge(v_mm, 2 * (2 * r + j))
                        take_x(r + j, 1 - j)
                    middle(3)
            peeled(act, n_iter, body)

        @block.vector
        def _(dve):
            dve.wait_ge(w_loaded, 16 * 12)
            dve.wait_ge(v_pad, 1)

            def body(r, first, last):
                for j in range(2):
                    for m in range(4):
                        n = 4 * (2 * r + j) + m
                        dve.wait_ge(full_ready, n + 1)
                        if m >= 2 or j or not first:
                            dve.wait_ge(part_saved[m % 2], 16 * (2 * (2 * r + j) + m // 2))
                        dve.tensor_copy(parts[:, m % 2, 0], full[:, m % 2]).then_inc(hi_ready, 1)
                        dve.wait_ge(hi_ready, n + 1)
                        if m >= 2 or j or not first:
                            dve.wait_ge(lo_ready, n - 1)
                        dve.tensor_tensor(rest[:, m % 2], full[:, m % 2], parts[:, m % 2, 0], ALU.subtract) \
                            .then_inc(rest_ready, 1)
                    for h in range(2):
                        dve.wait_ge(v_mm, 2 * (2 * r + j) + h + 1)
                        if j or not first:
                            dve.wait_ge(v_saved[h], 16 * 4 * (2 * r + j))
                        dve.tensor_tensor(
                            v_out[:, h, :, :, 0:HD].rearrange("p t h c -> p (t h) c"),
                            v_ps[:, h].rearrange("p t (h c) -> p (t h) c", c=HD),
                            pv0[:, :].unsqueeze(1).to_broadcast([P, 2 * dim // HD, HD]), ALU.add).then_inc(v_ready, 1)
            peeled(dve, n_iter, body)


def attention(nc, qk_scr, v_scr, pek, pev, attn):
    n_iter, seq, width = attn.shape
    QB = seq // P
    TILES = 2 * QB
    DEPTH = 5
    VW = 2 * HD
    assert QB == 8 and width == 2 * GRP * HD and BAND == 3 * P
    with ExitStack() as ctx:
        sb = lambda n, s, d=F32: ctx.enter_context(nc.sbuf_tensor(n, s, d))
        ps = lambda n, s: ctx.enter_context(nc.psum_tensor(n, s, F32))
        sem = lambda n: ctx.enter_context(nc.semaphore(n))
        sem2 = lambda n: [sem(f"{n}{i}") for i in range(2)]
        bias_scr = nc.dram_tensor("bias_scr", (2, GRP, P * PW), F32).ap()
        prob_scr = nc.dram_tensor("prob_scr", (2, GRP, PPITCH), F32).ap()
        ident = sb("a_ident", [P, P])
        pk_in = sb("a_pk_in", [HD, MAXD + 1])
        pk_diff = sb("a_pk_diff", [HD, MAXD])
        pk_rest = sb("a_pk_rest", [HD, MAXD])
        pk_parts = sb("a_pk_parts", [HD, 3, MAXD], BF16)
        pk = sb("a_pk", [P, MAXD], BF16)
        pv_in = sb("a_pv_in", [P, 2, HD])
        pv_0 = sb("a_pv_0", [P, HD])
        pv = sb("a_pv", [P, 2, VW])
        edge = sb("a_edge", [P, 2, P])
        q_s = sb("a_q", [P, 2, GRP, seq], BF16)
        k_s = sb("a_k", [P, 2, GRP, seq], BF16)
        v_s = sb("a_v", [P, 2, QB, GRP, VW])
        b_out = sb("a_b_out", [P, 2, GRP, MAXD])
        bias = sb("a_bias", [P, 2, GRP, BAND])
        neg_s = sb("a_neg_s", [P, 2, BAND])
        far_neg = sb("a_far_neg", [P, GRP])
        band_neg = sb("a_band_neg", [P, GRP])
        neg_max = sb("a_neg_max", [P, GRP])
        prob = sb("a_prob", [P, 2, GRP, MAXD + seq])
        sums = sb("a_sums", [P, QB, GRP, 2])
        p_t = sb("a_p_t", [P, 2, GRP, seq])
        band = sb("a_band", [P, 2, GRP, MAXD])
        band_t = sb("a_band_t", [P, 2, GRP, MAXD])
        o_t = sb("a_o_t", [P, P])
        total = sb("a_total", [P, GRP])
        inverse = sb("a_inverse", [P, GRP])
        o_out = sb("a_o_out", [P, 2, GRP, HD])
        s_ps = ps("a_s_ps", [P, 2, seq])
        t_ps = ps("a_t_ps", [P, 2, 512])
        b_ps = ps("a_b_ps", [P, 2, MAXD])
        o_ps = ps("a_o_ps", [P, 4, P])
        id_zero, id_ready, set_ready = sem("a_id_zero"), sem("a_id_ready"), sem("a_set_ready")
        pe_loaded, pk_step, pk_placed, pv_ready = sem("a_pe_loaded"), sem("a_pk_step"), sem("a_pk_placed"), sem("a_pv_ready")
        edge_saved = sem("a_edge_saved")
        qk_loaded, v_loaded = sem2("a_qk_loaded"), sem2("a_v_loaded")
        b_mm, b_evac = sem("a_b_mm"), sem("a_b_evac")
        b_saved, b_loaded = sem2("a_b_saved"), sem2("a_b_loaded")
        qk_mm, part_max, max_ready, exp_ready = sem("a_qk_mm"), sem("a_part_max"), sem("a_max_ready"), sem("a_exp_ready")
        p_saved, p_loaded = sem2("a_p_saved"), sem2("a_p_loaded")
        t_mm, r_mm = sem("a_t_mm"), sem("a_r_mm")
        t_evac = {"act": sem("a_t_evac_act"), "dve": sem("a_t_evac_dve")}
        r_evac = sem("a_r_evac")
        o_mm, o_evac, ot_mm = sem("a_o_mm"), sem("a_o_evac"), sem("a_ot_mm")
        sum_ready, inv_ready, out_ready = sem("a_sum_ready"), sem("a_inv_ready"), sem("a_out_ready")
        stored = sem2("a_stored")
        block = ctx.enter_context(nc.Block())

        def upto(per_tile, r, k):
            whole = sum(per_tile(t % QB) for t in range(TILES))
            return r * whole + (k // TILES) * whole + sum(per_tile(t % QB) for t in range(k % TILES))

        def t_banks(qb):
            return [range(b, min(b + 4, qb + 1)) for b in range(0, qb + 1, 4)]

        def t_engine(qb, u, i):
            return ("dve", "act")[i if qb >= 4 else u % 2]


        def t_done(eng, r, k, u, i):
            banks = lambda qb: [(h, b) for h in range(GRP) for b in range(len(t_banks(qb))) if t_engine(qb, h, b) == eng]
            of_tile = banks(k % QB)
            return upto(lambda qb: len(banks(qb)), r, k) + (len(of_tile) if i < 0 else of_tile.index((u, i)) + 1)

        def t_made(r, k, u):
            return upto(lambda qb: GRP * len(t_banks(qb)), r, k) + (u + 1) * len(t_banks(k % QB))

        def pair(r, k):
            return 16 * (QB * r + k // 2 + 1)

        def plan(k, first, last):
            jobs = []
            ok = lambda kk: (kk >= 0 or not first) and (kk < TILES or not last)
            for u in range(GRP):
                if ok(k - 1):
                    jobs += [("p", k - 1, u, i) for i in range(len(t_banks((k - 1) % QB)))]
                if ok(k - 2) and u < 2:
                    jobs.append(("band", k - 2, u, 0))
            return jobs

        def wait_evac(eng, r, job):
            kind, kk, u, i = job
            if kind == "p":
                who = t_engine(kk % QB, u, i)
                eng.wait_ge(t_evac[who], t_done(who, r, kk, u, i))
            else:
                eng.wait_ge(r_evac, 2 * (TILES * r + kk) + u + 1)

        def steps(first, last):
            return range(-2 if first else 0, TILES + (DEPTH - 1 if last else 0))

        def valid(kk, first, last):
            return (kk >= 0 or not first) and (kk < TILES or not last)

        def ahead(k, u, last):
            k, u = k + (u + 1) // GRP, (u + 1) % GRP
            return (k, u) if k >= 0 and (k < TILES or not last) else None

        def read_out(eng, copy, name, r, k, u, first, last):
            for pos, (kind, kk, uu, i) in enumerate(plan(k, first, last)):
                if uu != u:
                    continue
                par = kk % 2
                if kind == "p" and t_engine(kk % QB, u, i) == name:
                    blocks = t_banks(kk % QB)[i]
                    eng.wait_ge(t_mm, t_made(r, kk, u) - len(t_banks(kk % QB)) + i + 1)
                    if valid(kk - 2, first, last):
                        eng.wait_ge(o_mm, TILES * r + kk - 1)
                    copy(p_t[:, par, u, blocks[0] * P:(blocks[-1] + 1) * P], t_ps[:, pos % 2, 0:len(blocks) * P]) \
                        .then_inc(t_evac[name], 1)
                if kind == "band" and name == "dve":
                    eng.wait_ge(r_mm, 2 * (TILES * r + kk) + u + 1)
                    if valid(kk - 2, first, last):
                        eng.wait_ge(o_mm, TILES * r + kk - 1)
                    copy(band_t[:, par, 2 * u:2 * u + 2].rearrange("p h j -> p (h j)"), t_ps[:, pos % 2]) \
                        .then_inc(r_evac, 1)

        @block.sync
        def _(sp):
            sp.dma_start(pk_in[:, :], pek[0:MAXD + 1, :].rearrange("j d -> d j"), allow_slow_non_contiguous=True).then_inc(pe_loaded, 16)
            sp.dma_start(pv_in[:, :, :], pev[1:MAXD + 1, :].rearrange("(b p) d -> p b d", p=P)).then_inc(pe_loaded, 16)
            sp.dma_start(pv_0[:, :], pev[0:1, :].to_broadcast([P, HD])).then_inc(pe_loaded, 16)

            def load_qk(r, g):
                rows = slice(g * GRP * HD, (g + 1) * GRP * HD)
                for dst, which, terms in ((q_s, 0, TERMS_Q), (k_s, 1, TERMS_K)):
                    for i, part in enumerate(terms):
                        sp.dma_start(dst[i * HD:(i + 1) * HD, g], qk_scr[which, r, part, rows, :]
                                     .rearrange("(h d) t -> d h t", d=HD)).then_inc(qk_loaded[g], 16)

            def load_v(r, g):
                sp.dma_start(v_s[:, g].rearrange("p b h c -> p b (h c)"),
                             v_scr[2 * r + g].rearrange("(b p) c -> p b c", p=P)).then_inc(v_loaded[g], 16)

            load_qk(0, 0)
            load_v(0, 0)
            sp.wait_ge(set_ready, 5)
            for slot in range(2):
                rows = bias_scr[slot].rearrange("h (q c) -> q h c", c=PW)
                for i, at in ((0, 0), (1, P + MAXD)):
                    sp.dma_start(rows[:, :, at:at + P], edge[:, i].unsqueeze(1).to_broadcast([P, GRP, P])) \
                        .then_inc(edge_saved, 16)
            sp.wait_ge(pk_step, 5)
            for i, part in enumerate(TERMS_K):
                sp.dma_start(pk[i * HD:(i + 1) * HD, :], pk_parts[:, part]).then_inc(pk_placed, 16)
            sp.wait_ge(edge_saved, 16 * 4)

            def body(r, first, last):
                r_prev = r - 1 if first or last else sp.snap(r - 1)
                r_next = r + 1 if first or last else sp.snap(r + 1)
                for k in steps(first, last):
                    ok = lambda kk: valid(kk, first, last)
                    T = TILES * r + k
                    if k + 1 >= 0 and ok(k + 1):
                        par = (k + 1) % 2
                        sp.wait_ge(b_saved[par], pair(r, k + 1))
                        src = bias_scr[par][:, P - 1:P - 1 + P * (PW - 1)].rearrange("h (q c) -> q h c", c=PW - 1)
                        sp.dma_start(bias[:, par], src[:, :, 0:BAND]).then_inc(b_loaded[par], 16)
                    if k >= 0 and ok(k - 1) and k - 1 < TILES:
                        par = (k - 1) % 2
                        sp.wait_ge(p_saved[par], pair(r, k - 1))
                        src = prob_scr[par][:, 1:1 + P * (BAND + 1)].rearrange("h (q c) -> q h c", c=BAND + 1)
                        sp.dma_start(band[:, par], src[:, :, 0:MAXD]).then_inc(p_loaded[par], 16)
                    g_next = k // QB + 1
                    if 0 <= k < TILES and (g_next == 1 or not last):
                        if k % QB == 0:
                            if ok(k - 1):
                                sp.wait_ge(qk_mm, 4 * TILES * r + 4 * k)
                            load_qk(r_next if g_next == 2 else r, g_next % 2)
                        if k % QB == 3:
                            if ok(k - 4):
                                sp.wait_ge(o_mm, T - 3)
                            load_v(r_next if g_next == 2 else r, g_next % 2)
                    if k >= 0 and ok(k - 4):
                        par = (k - 4) % 2
                        qb, g = (k - 4) % QB, ((k - 4) % TILES) // QB
                        sp.wait_ge(out_ready, T - 3)
                        row = attn[r_prev if k < 4 else r]
                        sp.dma_start(row[qb * P:(qb + 1) * P, g * GRP * HD:(g + 1) * GRP * HD],
                                     o_out[:, par].rearrange("p h d -> p (h d)")).then_inc(stored[par], 16)
                    if ok(k + 2):
                        par = k % 2
                        sp.wait_ge(b_evac, 2 * TILES * r + 2 * k + 6)
                        if k >= 0:
                            sp.wait_ge(b_loaded[par], pair(r, k))
                        rows = bias_scr[par].rearrange("h (q c) -> q h c", c=PW)
                        sp.dma_start(rows[:, :, P:P + MAXD], b_out[:, par]).then_inc(b_saved[par], 16)
                    if 0 <= k < TILES:
                        par, qb = k % 2, k % QB
                        sp.wait_ge(exp_ready, 4 * TILES * r + 4 * k + 4)
                        if ok(k - 2):
                            sp.wait_ge(p_loaded[par], pair(r, k - 2))
                        rows = prob_scr[par][:, 0:P * BAND].rearrange("h (q c) -> q h c", c=BAND)
                        sp.dma_start(rows, prob[:, par, :, qb * P:qb * P + BAND]).then_inc(p_saved[par], 16)
            peeled(sp, n_iter, body)
            for par in range(2):
                sp.wait_ge(stored[par], 16 * QB * n_iter)
                sp.wait_ge(b_saved[par], 16 * QB * n_iter)
                sp.wait_ge(p_saved[par], 16 * QB * n_iter)

        @block.gpsimd
        def _(pool):
            pool.memset(edge[:, 0], 0.0).then_inc(set_ready, 1)
            pool.memset(edge[:, 1], NEG).then_inc(set_ready, 1)
            pool.memset(pv[:, :, HD:VW], 0.0).then_inc(set_ready, 1)
            pool.memset(sums[:, :, :, :], 0.0).then_inc(set_ready, 1)
            pool.memset(prob[:, :, :, 0:MAXD], 0.0).then_inc(set_ready, 1)
            pool.memset(ident[:, :], 0.0).then_inc(id_zero, 1)
            pool.wait_ge(id_zero, 1)
            pool.affine_select(out=ident[:, :], in_=ident[:, :], compare_op=ALU.not_equal, fill=1.0, base=0,
                               pattern=[[-1, P]], channel_multiplier=1).then_inc(id_ready, 1)

        @block.tensor
        def _(pe):
            pe.wait_ge(id_ready, 1)
            pe.wait_ge(pk_placed, 16 * len(TERMS_K))
            pe.wait_ge(pv_ready, 1)

            def scores(r, k, u, first, last):
                g, qb = (k // QB) % 2, k % QB
                unit = 4 * (TILES * r + k) + u
                if not (first and 4 * k + u < 2):
                    pe.wait_ge(exp_ready, unit - 1)
                for c in range(0, (qb + 1) * P, 512):
                    e = min(c + 512, (qb + 1) * P)
                    mm = pe.matmul(s_ps[:, u % 2, c:e], q_s[0:ROWS, g, u, qb * P:(qb + 1) * P],
                                   k_s[0:ROWS, g, u, c:e], start=True, stop=True)
                mm.then_inc(qk_mm, 1)

            def biases(r, k, c, first):
                g, qb = (k // QB) % 2, k % QB
                if qb == 0 and c == 0:
                    pe.wait_ge(qk_loaded[g], 16 * 12 * (r + k // TILES + 1))
                if not (first and k == 0 and c == 0):
                    pe.wait_ge(b_evac, 2 * (TILES * r + k) + c)
                for h in range(2):
                    mm = pe.matmul(b_ps[:, h], q_s[0:ROWS, g, 2 * c + h, qb * P:(qb + 1) * P], pk[0:ROWS, :],
                                   start=(h == 0), stop=True, skip_group_check=True)
                mm.then_inc(b_mm, 1)

            def values(r, k, first, last):
                g, qb, par = (k // QB) % 2, k % QB, k % 2
                for name in ("act", "dve"):
                    pe.wait_ge(t_evac[name], t_done(name, r, k, 0, -1))
                pe.wait_ge(r_evac, 2 * (TILES * r + k) + 2)
                if qb == 0:
                    pe.wait_ge(v_loaded[g], 16 * (r + k // TILES + 1))
                if valid(k - 1, first, last):
                    pe.wait_ge(out_ready, TILES * r + k)
                for j in range(qb + 1 + 2):
                    for h in range(GRP):
                        if j <= qb:
                            w, m = v_s[:, g, j, h], p_t[:, par, h, j * P:(j + 1) * P]
                        else:
                            w, m = pv[:, j - qb - 1], band_t[:, par, h, (j - qb - 1) * P:(j - qb) * P]
                        mm = pe.matmul(o_ps[h * VW:(h + 1) * VW, 0], w, m, start=(j == 0), stop=(j == qb + 2))
                mm.then_inc(o_mm, 1)

            def body(r, first, last):
                for k in steps(first, last):
                    ok = lambda kk: valid(kk, first, last)
                    jobs = plan(k, first, last)
                    earlier = plan(k - 1, first, last)[-2:]
                    for u in range(GRP):
                        if ahead(k, u, last):
                            scores(r, *ahead(k, u, last), first, last)
                        if ok(k + 2) and u % 2 == 0:
                            biases(r, k + 2, u // 2, first)
                        if u == 1 and ok(k - 3) and k >= 0:
                            pe.wait_ge(o_evac, TILES * r + k - 2)
                            pe.transpose(o_ps[:, 2], o_t[:, :], ident[:, :]).then_inc(ot_mm, 1)
                        for pos, job in enumerate(jobs):
                            kind, kk, uu, i = job
                            if uu != u:
                                continue
                            before = jobs[pos - 2] if pos >= 2 else (earlier[pos] if earlier else None)
                            if before:
                                wait_evac(pe, r, before)
                            if kind == "p":
                                pe.wait_ge(exp_ready, 4 * (TILES * r + kk) + u + 1)
                                for n, b in enumerate(t_banks(kk % QB)[i]):
                                    mm = pe.transpose(t_ps[:, pos % 2, n * P:(n + 1) * P],
                                                      prob[:, kk % 2, u, MAXD + b * P:MAXD + (b + 1) * P], ident[:, :])
                                mm.then_inc(t_mm, 1)
                            else:
                                pe.wait_ge(p_loaded[kk % 2], pair(r, kk))
                                for n in range(4):
                                    mm = pe.transpose(t_ps[:, pos % 2, n * P:(n + 1) * P],
                                                      band[:, kk % 2, 2 * u + n // 2, (n % 2) * P:(n % 2 + 1) * P],
                                                      ident[:, :])
                                mm.then_inc(r_mm, 1)
                    if ok(k - 2) and 0 <= k < TILES + 2:
                        values(r, k - 2, first, last)
            peeled(pe, n_iter, body)

        @block.scalar
        def _(act):
            act.wait_ge(set_ready, 5)

            def body(r, first, last):
                for k in steps(first, last):
                    ok = lambda kk: valid(kk, first, last)
                    T = TILES * r + k
                    for u in range(GRP):
                        if 0 <= k < TILES:
                            par, qb = k % 2, k % QB
                            lo = max(0, qb - 2) * P
                            w = (qb + 1) * P - lo
                            if ok(k - 2):
                                act.wait_ge(t_mm, t_made(r, k - 2, u))
                                if u == 0:
                                    act.wait_ge(p_saved[par], pair(r, k - 2))
                            act.wait_ge(max_ready, 4 * T + u + 1)
                            e = act.activation(prob[:, par, u, MAXD + lo:MAXD + lo + w], neg_s[:, u % 2, 0:w], ACT.Exp,
                                               bias=neg_max[:, u:u + 1], scale=-1.0, accum_out=sums[:, qb, u, 0:1])
                            if lo:
                                e = act.activation(prob[:, par, u, MAXD:MAXD + lo], s_ps[:, u % 2, 0:lo], ACT.Exp,
                                                   bias=neg_max[:, u:u + 1], accum_out=sums[:, qb, u, 1:2])
                            e.then_inc(exp_ready, 1)
                        if ok(k + 2) and u % 2 == 0:
                            act.wait_ge(b_mm, 2 * (T + 2) + u // 2 + 1)
                            if u == 0 and k >= 0:
                                act.wait_ge(b_saved[k % 2], pair(r, k))
                            act.activation(b_out[:, k % 2, u:u + 2], b_ps[:, :, :], ACT.Copy).then_inc(b_evac, 1)
                        if u == 0 and ok(k - 3) and k >= 0:
                            act.wait_ge(o_mm, T - 2)
                            if ok(k - 4):
                                act.wait_ge(ot_mm, T - 3)
                            act.activation(o_t[:, :], o_ps[:, 0], ACT.Copy).then_inc(o_evac, 1)
                        read_out(act, lambda o, i: act.activation(o, i, ACT.Copy), "act", r, k, u, first, last)
            peeled(act, n_iter, body)

        @block.vector
        def _(dve):
            dve.wait_ge(pe_loaded, 16 * 3)
            dve.wait_ge(set_ready, 5)
            dve.tensor_scalar(pk_diff[:, :], pk_in[:, 1:MAXD + 1], pk_in[:, 0:1], None, ALU.subtract).then_inc(pk_step, 1)
            dve.tensor_tensor(pv[:, :, 0:HD], pv_in[:, :, :], pv_0[:, :].unsqueeze(1).to_broadcast([P, 2, HD]),
                              ALU.subtract).then_inc(pv_ready, 1)
            dve.wait_ge(pk_step, 1)
            dve.tensor_copy(pk_parts[:, 0], pk_diff[:, :]).then_inc(pk_step, 1)
            dve.wait_ge(pk_step, 2)
            dve.tensor_tensor(pk_rest[:, :], pk_diff[:, :], pk_parts[:, 0], ALU.subtract).then_inc(pk_step, 1)
            dve.wait_ge(pk_step, 3)
            dve.tensor_copy(pk_parts[:, 1], pk_rest[:, :]).then_inc(pk_step, 1)
            dve.wait_ge(pk_step, 4)
            dve.tensor_tensor(pk_parts[:, 2], pk_rest[:, :], pk_parts[:, 1], ALU.subtract).then_inc(pk_step, 1)

            def maximum(r, k, u):
                par, qb, T = k % 2, k % QB, TILES * r + k
                lo = max(0, qb - 2) * P
                w = (qb + 1) * P - lo
                dve.wait_ge(qk_mm, 4 * T + u + 1)
                if u == 0:
                    dve.wait_ge(b_loaded[par], pair(r, k))
                if lo:
                    dve.tensor_reduce(far_neg[:, u:u + 1], s_ps[:, u % 2, 0:lo], AX.X, ALU.max,
                                      negate=True).then_inc(part_max, 1)
                else:
                    dve.memset(far_neg[:, u:u + 1], BIG).then_inc(part_max, 1)
                dve.tensor_tensor_reduce(neg_s[:, u % 2, 0:w], s_ps[:, u % 2, lo:lo + w],
                                         bias[:, par, u, BAND - w:BAND], -1.0, BIG, ALU.add, ALU.min,
                                         accum_out=band_neg[:, u:u + 1]).then_inc(part_max, 1)
                dve.wait_ge(part_max, 8 * T + 2 * u + 2)
                dve.tensor_tensor(neg_max[:, u:u + 1], far_neg[:, u:u + 1], band_neg[:, u:u + 1], ALU.min) \
                    .then_inc(max_ready, 1)

            def body(r, first, last):
                for k in steps(first, last):
                    ok = lambda kk: valid(kk, first, last)
                    T = TILES * r + k
                    for u in range(GRP):
                        if ahead(k, u, last):
                            maximum(r, *ahead(k, u, last))
                        read_out(dve, dve.tensor_copy, "dve", r, k, u, first, last)
                        if u == 2 and ok(k - 3) and k >= 0:
                            par, qb = (k - 3) % 2, (k - 3) % QB
                            dve.wait_ge(ot_mm, T - 2)
                            dve.tensor_tensor(total[:, :], sums[:, qb, :, 0], sums[:, qb, :, 1], ALU.add).then_inc(sum_ready, 1)
                            dve.wait_ge(sum_ready, T - 2)
                            dve.reciprocal(inverse[:, :], total[:, :]).then_inc(inv_ready, 1)
                            dve.wait_ge(inv_ready, T - 2)
                            if ok(k - 5):
                                dve.wait_ge(stored[par], pair(r, k - 5))
                            dve.tensor_tensor(o_out[:, par], o_ps[:, 2].rearrange("p (h c) -> p h c", c=VW)[:, :, 0:HD],
                                              inverse[:, :].unsqueeze(2).to_broadcast([P, GRP, HD]), ALU.mult) \
                                .then_inc(out_ready, 1)
            peeled(dve, n_iter, body)


def feed_forward(nc, x, attn, wo, wg, wu, wd, out):
    nb, seq, dim = x.shape
    hid = wg.shape[0]
    HC = hid // P
    assert dim == 2 * P and HC == 6 and seq == 2 * CHUNK
    x_d, a_d, o_d = (t.rearrange("b (c t p) d -> b c p t d", p=P, t=CT) for t in (x, attn, out))
    with ExitStack() as ctx:
        sb = lambda n, s, d=F32: ctx.enter_context(nc.sbuf_tensor(n, s, d))
        ps = lambda n, s: ctx.enter_context(nc.psum_tensor(n, s, F32))
        sem = lambda n: ctx.enter_context(nc.semaphore(n))
        ident = sb("f_ident", [P, P])
        wo_in = sb("f_wo_in", [P, 2, dim])
        w_int = sb("f_w_int", [P, 2, HC, dim], I32)
        wd_int = sb("f_wd_int", [P, 2, hid], I32)
        wo_t = sb("f_wo_t", [P, 2, dim])
        w_t = sb("f_w_t", [P, 2, 2, hid])
        wd_t = sb("f_wd_t", [P, HC, dim])
        eps = sb("f_eps", [P, CT])
        neg_half = sb("f_neg_half", [P, CT])
        half = sb("f_half", [P, CT])
        inv_dim = sb("f_inv_dim", [P, CT])
        x_in = sb("f_x_in", [P, 2, CT, dim])
        a_in = sb("f_a_in", [P, 2, CT, dim])
        a_t = sb("f_a_t", [P, 2, CHUNK])
        x1 = sb("f_x1", [P, CT, dim])
        z = sb("f_z", [P, 2, CT, dim])
        z_t = sb("f_z_t", [P, 2, CHUNK])
        gate = sb("f_gate", [P, 2, CHUNK])
        h_t = sb("f_h_t", [P, HC, CHUNK])
        x2 = sb("f_x2", [P, CT, dim])
        o_out = sb("f_o_out", [P, 2, CT, dim])
        stats = sb("f_stats", [P, 2, CT, 6])
        half_mean, half_diff, sq_sum = (sb(f"f_{n}", [P, 2, CT]) for n in ("half_mean", "half_diff", "sq_sum"))
        mean, diff, var_in, var_between, var, var_eps, rstd = (
            sb(f"f_{n}", [P, 2, CT]) for n in ("mean", "diff", "var_in", "var_between", "var", "var_eps", "rstd"))
        tr_ps = ps("f_tr_ps", [P, 2, CHUNK])
        y_ps = ps("f_y_ps", [P, 2, 2, dim])
        g_ps = ps("f_g_ps", [P, 2, CHUNK])
        u_ps = ps("f_u_ps", [P, 2, CHUNK])
        id_zero, id_ready, const_ready = sem("f_id_zero"), sem("f_id_ready"), sem("f_const_ready")
        w_loaded, w_cast, w_tr, w_ready = sem("f_w_loaded"), sem("f_w_cast"), sem("f_w_tr"), sem("f_w_ready")
        in_loaded = [sem(f"f_in_loaded{i}") for i in range(2)]
        at_mm, at_ready = sem("f_at_mm"), sem("f_at_ready")
        y_mm, y_taken = sem("f_y_mm"), sem("f_y_taken")
        d_mm, d_taken = sem("f_d_mm"), sem("f_d_taken")
        stat = [sem(f"f_stat{k}") for k in range(2)]
        ln_step = [sem(f"f_ln_step{k}") for k in range(2)]
        normed = [sem(f"f_normed{k}") for k in range(2)]
        zt_mm, zt_ready = sem("f_zt_mm"), sem("f_zt_ready")
        g_mm, g_ready, h_ready = sem("f_g_mm"), sem("f_g_ready"), sem("f_h_ready")
        stored = [sem(f"f_stored{i}") for i in range(2)]
        block = ctx.enter_context(nc.Block())
        LN_STEPS = 10

        def weight_jobs():
            for c in range(2):
                yield wo_t[:, c], [wo_in[:, t, c * P:(c + 1) * P] for t in range(2)]
            for i in range(2):
                for c in range(2):
                    for s in (0, 3):
                        yield (w_t[:, i, c, s * P:(s + 3) * P],
                               [w_int[:, i, t, c * P:(c + 1) * P].bitcast(F32) for t in range(s, s + 3)])
            for h in range(HC):
                yield wd_t[:, h], [wd_int[:, t, h * P:(h + 1) * P].bitcast(F32) for t in range(2)]

        @block.sync
        def _(sp):
            sp.dma_start(wo_in[:, :, :], wo.rearrange("(t p) d -> p t d", p=P)).then_inc(w_loaded, 16)
            for i, w in enumerate((wg, wu)):
                sp.dma_start(w_int[:, i], w.rearrange("(t p) d -> p t d", p=P)).then_inc(w_loaded, 16)
            sp.dma_start(wd_int[:, :, :], wd.rearrange("(t p) d -> p t d", p=P)).then_inc(w_loaded, 16)

            def load(r, j):
                sp.dma_start(x_in[:, j], x_d[r, j]).then_inc(in_loaded[j], 16)
                for k in range(2):
                    sp.dma_start(a_in[:, j, :, k * P:(k + 1) * P], a_d[2 * r + k, j]).then_inc(in_loaded[j], 16)

            load(0, 0)
            load(0, 1)

            def body(r, first, last):
                for j in range(2):
                    c = 2 * r + j
                    if not last:
                        sp.wait_ge(at_mm, 2 * c + 2)
                        sp.wait_ge(y_taken, 2 * c + 2)
                        load(r + 1, j)
                    sp.wait_ge(normed[1], 4 * c + 4)
                    sp.dma_start(o_d[r, j], o_out[:, j]).then_inc(stored[j], 16)
            peeled(sp, nb, body)
            for j in range(2):
                sp.wait_ge(stored[j], 16 * nb)

        @block.gpsimd
        def _(pool):
            pool.memset(ident[:, :], 0.0).then_inc(id_zero, 1)
            pool.wait_ge(id_zero, 1)
            pool.affine_select(out=ident[:, :], in_=ident[:, :], compare_op=ALU.not_equal, fill=1.0, base=0,
                               pattern=[[-1, P]], channel_multiplier=1).then_inc(id_ready, 1)
            pool.memset(eps[:, :], EPS).then_inc(const_ready, 1)
            pool.memset(neg_half[:, :], -0.5).then_inc(const_ready, 1)
            pool.memset(half[:, :], 0.5).then_inc(const_ready, 1)
            pool.memset(inv_dim[:, :], 1.0 / dim).then_inc(const_ready, 1)
            pool.wait_ge(const_ready, 4)

            def moments(c, k):
                pool.wait_ge(stat[k], 4 * c + 4)
                base = LN_STEPS * c
                s = stats[:, k]
                inc = lambda ins: ins.then_inc(ln_step[k], 1)
                inc(pool.tensor_tensor(half_mean[:, k], s[:, :, 1], s[:, :, 4], ALU.add))
                inc(pool.tensor_tensor(half_diff[:, k], s[:, :, 1], s[:, :, 4], ALU.subtract))
                inc(pool.tensor_tensor(sq_sum[:, k], s[:, :, 2], s[:, :, 5], ALU.add))
                pool.wait_ge(ln_step[k], base + 3)
                inc(pool.tensor_tensor(mean[:, k], half_mean[:, k], half[:, :], ALU.mult))
                inc(pool.tensor_tensor(diff[:, k], half_diff[:, k], half[:, :], ALU.mult))
                inc(pool.tensor_tensor(var_in[:, k], sq_sum[:, k], inv_dim[:, :], ALU.mult))
                pool.wait_ge(ln_step[k], base + 6)
                inc(pool.tensor_tensor(var_between[:, k], diff[:, k], diff[:, k], ALU.mult))
                pool.wait_ge(ln_step[k], base + 7)
                inc(pool.tensor_tensor(var[:, k], var_in[:, k], var_between[:, k], ALU.add))
                pool.wait_ge(ln_step[k], base + 8)
                inc(pool.tensor_tensor(var_eps[:, k], var[:, k], eps[:, :], ALU.add))
                pool.wait_ge(ln_step[k], base + 9)
                inc(pool.tensor_tensor(rstd[:, k], var_eps[:, k], neg_half[:, :], ALU.pow))

            moments(0, 0)

            def body(r, first, last):
                for j in range(2):
                    if j == 0 or not last:
                        moments(2 * r + j + 1, 0)
                    moments(2 * r + j, 1)
            peeled(pool, nb, body)

        @block.tensor
        def _(pe):
            pe.wait_ge(id_ready, 1)
            pe.wait_ge(w_loaded, 16 * 4)
            pe.wait_ge(w_cast, 3)
            for n, (_, pieces) in enumerate(weight_jobs()):
                if n >= 2:
                    pe.wait_ge(w_ready, n - 1)
                for t, piece in enumerate(pieces):
                    mm = pe.transpose(tr_ps[:, n % 2, t * P:(t + 1) * P], piece, ident[:, :])
                mm.then_inc(w_tr, 1)
            pe.wait_ge(w_ready, n + 1)

            def attn_transposes(r, j, c):
                pe.wait_ge(in_loaded[j], 48 * r + 48)
                for k in range(2):
                    for t in range(CT):
                        mm = pe.transpose(tr_ps[:, k, t * P:(t + 1) * P], a_in[:, j, t, k * P:(k + 1) * P], ident[:, :])
                    mm.then_inc(at_mm, 1)

            def attn_output(c):
                pe.wait_ge(at_ready, 2 * c + 2)
                for b in range(2):
                    for t in range(2):
                        for k in range(2):
                            mm = pe.matmul(y_ps[:, b, t], a_t[:, k, (2 * b + t) * P:(2 * b + t + 1) * P], wo_t[:, k],
                                           start=(t == 0 and k == 0), stop=(k == 1), skip_group_check=True)
                    mm.then_inc(y_mm, 1)

            def z_transposes(j, c):
                for t in range(CT):
                    pe.wait_ge(normed[0], 4 * c + t + 1)
                    for k in range(2):
                        mm = pe.transpose(tr_ps[:, k, t * P:(t + 1) * P], z[:, j, t, k * P:(k + 1) * P], ident[:, :])
                        if t == CT - 1:
                            mm.then_inc(zt_mm, 1)

            attn_transposes(0, 0, 0)
            attn_output(0)
            z_transposes(0, 0)

            def body(r, first, last):
                for j in range(2):
                    c = 2 * r + j
                    more = j == 0 or not last

                    def hidden(m):
                        n = HC * c + m
                        if m >= 2 or j or not first:
                            pe.wait_ge(h_ready, n - 1)
                        for ps_, i in ((g_ps, 0), (u_ps, 1)):
                            for k in range(2):
                                mm = pe.matmul(ps_[:, m % 2], w_t[:, i, k, m * P:(m + 1) * P], z_t[:, k],
                                               start=(k == 0), stop=(k == 1))
                        mm.then_inc(g_mm, 1)

                    pe.wait_ge(zt_ready, 2 * c + 2)
                    for m in range(3):
                        hidden(m)
                    if more:
                        attn_transposes(r + j, 1 - j, c + 1)
                    hidden(3)
                    if more:
                        if j or not first:
                            pe.wait_ge(d_taken, 2 * c)
                        attn_output(c + 1)
                    hidden(4)
                    hidden(5)
                    if more:
                        pe.wait_ge(y_taken, 2 * c + 4)
                    for m in range(HC):
                        for b in range(2):
                            for t in range(2):
                                if b == 0 and t == 0:
                                    pe.wait_ge(h_ready, HC * c + m + 1)
                                mm = pe.matmul(y_ps[:, b, t], h_t[:, m, (2 * b + t) * P:(2 * b + t + 1) * P],
                                               wd_t[:, m], start=(m == 0 and t == 0), stop=(m == HC - 1),
                                               skip_group_check=True)
                            if m == HC - 1:
                                mm.then_inc(d_mm, 1)
                    if more:
                        z_transposes(1 - j, c + 1)
            peeled(pe, nb, body)

        @block.scalar
        def _(act):
            for n, (dst, pieces) in enumerate(weight_jobs()):
                act.wait_ge(w_tr, n + 1)
                act.activation(dst, tr_ps[:, n % 2, 0:P * len(pieces)], ACT.Copy).then_inc(w_ready, 1)

            def take(mm, ready, dst, c):
                for k in range(2):
                    act.wait_ge(mm, 2 * c + k + 1)
                    act.activation(dst[:, k], tr_ps[:, k], ACT.Copy).then_inc(ready, 1)

            take(at_mm, at_ready, a_t, 0)
            take(zt_mm, zt_ready, z_t, 0)

            def body(r, first, last):
                for j in range(2):
                    c = 2 * r + j
                    for m in range(HC):
                        n = HC * c + m
                        act.wait_ge(g_mm, n + 1)
                        if m >= 2 or j or not first:
                            act.wait_ge(h_ready, n - 1)
                        act.activation(gate[:, m % 2], g_ps[:, m % 2], ACT.Silu).then_inc(g_ready, 1)
                        if m == 2 and (j == 0 or not last):
                            take(at_mm, at_ready, a_t, c + 1)
                    if j == 0 or not last:
                        take(zt_mm, zt_ready, z_t, c + 1)
            peeled(act, nb, body)

        @block.vector
        def _(dve):
            dve.wait_ge(w_loaded, 16 * 4)
            for src in (w_int[:, 0], w_int[:, 1], wd_int):
                src = src[:, :, :]
                dve.tensor_scalar(src.bitcast(F32), src, W_SCALE, None, ALU.mult).then_inc(w_cast, 1)

            def residual(mm, taken, dst, other, c):
                for b in range(2):
                    dve.wait_ge(mm, 2 * c + b + 1)
                    dve.tensor_tensor(dst[:, 2 * b:2 * b + 2], other[:, 2 * b:2 * b + 2], y_ps[:, b], ALU.add) \
                        .then_inc(taken, 1)

            def norm(k, c, src, taken, dst):
                dve.wait_ge(taken, 2 * c + 2)
                for t in range(CT):
                    dve.bn_stats(stats[:, k, t], src[:, t]).then_inc(stat[k], 1)
                dve.wait_ge(ln_step[k], LN_STEPS * c + LN_STEPS)
                for t in range(CT):
                    dve.tensor_scalar(dst[:, t], src[:, t], mean[:, k, t:t + 1], rstd[:, k, t:t + 1],
                                      ALU.subtract, ALU.mult).then_inc(normed[k], 1)

            dve.wait_ge(in_loaded[0], 48)
            residual(y_mm, y_taken, x1, x_in[:, 0], 0)
            norm(0, 0, x1, y_taken, z[:, 0])

            def body(r, first, last):
                for j in range(2):
                    c = 2 * r + j
                    more = j == 0 or not last
                    for m in range(HC):
                        n = HC * c + m
                        if m == HC - 1 and more:
                            dve.wait_ge(in_loaded[1 - j], 48 * (r + j) + 48)
                            residual(y_mm, y_taken, x1, x_in[:, 1 - j], c + 1)
                        dve.wait_ge(g_ready, n + 1)
                        dve.tensor_tensor(h_t[:, m], gate[:, m % 2], u_ps[:, m % 2], ALU.mult).then_inc(h_ready, 1)
                    if more:
                        norm(0, c + 1, x1, y_taken, z[:, 1 - j])
                    residual(d_mm, d_taken, x2, z[:, j], c)
                    if not first:
                        dve.wait_ge(stored[j], 16 * r)
                    norm(1, c, x2, d_taken, o_out[:, j])
            peeled(dve, nb, body)


def build(nc, x, wq, wk, wv, wo, pek, pev, wg, wu, wd, out):
    nb, seq, dim = x.shape
    qk_scr = nc.dram_tensor("qk_scr", (2, nb * 2, 3, P, seq), BF16).ap()
    v_scr = nc.dram_tensor("v_scr", (nb * 4, seq, GRP * 2 * HD), F32).ap()
    attn = nc.dram_tensor("attn_scr", (nb * 2, seq, P), F32).ap()
    project(nc, x, wq, wk, wv, pek, pev, qk_scr, v_scr)
    attention(nc, qk_scr, v_scr, pek, pev, attn)
    feed_forward(nc, x, attn, wo, wg, wu, wd, out)


_INS = ["L0_attn_x", "L0_attn_Wq", "L0_attn_Wk", "L0_attn_Wv", "L0_attn_Wo", "L0_attn_pek", "L0_attn_pev",
        "L0_ffn_w_gate", "L0_ffn_w_up", "L0_ffn_w_down"]


def kernel(**inputs):
    import numpy as _np
    import concourse.bacc as _bacc
    from concourse import mybir as _mybir
    from concourse.bass_utils import run_bass_kernel_spmd as _run

    nc = _bacc.Bacc("TRN2", target_bir_lowering=False, num_devices=1)
    arrays, args = {}, []
    for name in _INS:
        a = _np.ascontiguousarray(inputs[name])
        arrays[f"in_{name}"] = a
        args.append(nc.dram_tensor(f"in_{name}", a.shape, _mybir.dt.from_np(a.dtype), kind="ExternalInput").ap())
    out = nc.dram_tensor("out_0", inputs["L0_attn_x"].shape, _mybir.dt.float32, kind="ExternalOutput").ap()
    build(nc, *args, out)
    r = _run(nc, [arrays], core_ids=[0])
    return r.results[0]["out_0"]
```

```python
from contextlib import ExitStack

import concourse.bass as bass
from concourse import mybir

ALU = mybir.AluOpType
ACT = mybir.ActivationFunctionType
F32 = mybir.dt.float32
BF16 = mybir.dt.bfloat16
I32 = mybir.dt.int32
AX = mybir.AxisListType

P = 128
HD = 16
MAXD = 256
GRP = 4
CHUNK = 512
CT = CHUNK // P
TERMS_Q = (0, 0, 1, 1, 0, 2)
TERMS_K = (0, 1, 0, 1, 2, 0)
ROWS = HD * len(TERMS_Q)
NEG = -1.0e30
BIG = 3.0e38
EPS = 1e-5
W_SCALE = 1.0 / 127.0
PW = 2 * P + MAXD
BAND = MAXD + P
PPITCH = P * BAND + MAXD


def peeled(eng, n, body):
    body(0, True, n == 1)
    if n > 2:
        with eng.Fori(1, n - 1) as i:
            body(i, False, False)
    if n > 1:
        body(n - 1, False, True)


def project(nc, x, wq, wk, wv, pek, pev, qk_scr, v_scr):
    nb, seq, dim = x.shape
    n_iter = nb
    assert seq == 2 * CHUNK and dim == 2 * P
    with ExitStack() as ctx:
        sb = lambda n, s, d=F32: ctx.enter_context(nc.sbuf_tensor(n, s, d))
        ps = lambda n, s: ctx.enter_context(nc.psum_tensor(n, s, F32))
        sem = lambda n: ctx.enter_context(nc.semaphore(n))
        ident = sb("p_ident", [P, P])
        w_in = sb("p_w_in", [P, 3, 2, dim])
        w_t = sb("p_w_t", [P, 3, 2, dim])
        pe0 = sb("p_pe0", [P, 1])
        pv0 = sb("p_pv0", [P, HD])
        x_in = sb("p_x_in", [P, 2, CT, dim])
        x_t = sb("p_x_t", [P, 2, 2, CHUNK])
        full = sb("p_full", [P, 2, CHUNK])
        rest = sb("p_rest", [P, 2, CHUNK])
        parts = sb("p_parts", [P, 2, 3, CHUNK], BF16)
        v_out = sb("p_v_out", [P, 2, 2, dim // HD, 2 * HD])
        tr_ps = ps("p_tr_ps", [P, 2, CHUNK])
        pr_ps = ps("p_pr_ps", [P, 2, CHUNK])
        v_ps = ps("p_v_ps", [P, 2, 2, dim])
        id_zero, id_ready = sem("p_id_zero"), sem("p_id_ready")
        w_loaded, w_tr, w_ready = sem("p_w_loaded"), sem("p_w_tr"), sem("p_w_ready")
        v_pad = sem("p_v_pad")
        x_loaded = [sem(f"p_x_loaded{i}") for i in range(2)]
        xt_mm, xt_ready = sem("p_xt_mm"), sem("p_xt_ready")
        pr_mm, full_ready = sem("p_pr_mm"), sem("p_full_ready")
        hi_ready, rest_ready, mid_ready, lo_ready = sem("p_hi"), sem("p_rest_ready"), sem("p_mid"), sem("p_lo")
        v_mm, v_ready = sem("p_v_mm"), sem("p_v_ready")
        part_saved = [sem(f"p_part_saved{i}") for i in range(2)]
        v_saved = [sem(f"p_v_saved{i}") for i in range(2)]
        block = ctx.enter_context(nc.Block())

        @block.sync
        def _(sp):
            for i, w in enumerate((wq, wk, wv)):
                sp.dma_start(w_in[:, i], w.rearrange("(t p) d -> p t d", p=P)).then_inc(w_loaded, 16)
            for h in range(P // HD):
                sp.dma_start(pe0[h * HD:(h + 1) * HD, :], pek[0:1, :].rearrange("a d -> d a")).then_inc(w_loaded, 16)
            sp.dma_start(pv0[:, :], pev[0:1, :].to_broadcast([P, HD])).then_inc(w_loaded, 16)

            def load(r, j):
                sp.dma_start(x_in[:, j], x[r, j * CHUNK:(j + 1) * CHUNK, :]
                             .rearrange("(t p) d -> p t d", p=P)).then_inc(x_loaded[j], 16)

            load(0, 0)

            def body(r, first, last):
                for j in range(2):
                    if j == 0 or not last:
                        if j or not first:
                            sp.wait_ge(xt_mm, 2 * (2 * r + j))
                        load(r + j, 1 - j)
                    for m in range(4):
                        sp.wait_ge(lo_ready, 4 * (2 * r + j) + m + 1)
                        sp.dma_start(qk_scr[m // 2, r * 2 + m % 2, :, :, j * CHUNK:(j + 1) * CHUNK]
                                     .rearrange("s p t -> p s t"), parts[:, m % 2]).then_inc(part_saved[m % 2], 16)
                    for h in range(2):
                        sp.wait_ge(v_ready, 2 * (2 * r + j) + h + 1)
                        for g in range(4):
                            sp.dma_start(
                                v_scr[r * 4 + g, j * CHUNK + h * 2 * P:j * CHUNK + (h + 1) * 2 * P, :]
                                .rearrange("(t p) c -> p t c", p=P),
                                v_out[:, h, :, g * GRP:(g + 1) * GRP, :].rearrange("p t h c -> p t (h c)")) \
                                .then_inc(v_saved[h], 16)
            peeled(sp, n_iter, body)
            for i in range(2):
                sp.wait_ge(part_saved[i], 16 * 4 * n_iter)
                sp.wait_ge(v_saved[i], 16 * 8 * n_iter)

        @block.gpsimd
        def _(pool):
            pool.memset(ident[:, :], 0.0).then_inc(id_zero, 1)
            pool.wait_ge(id_zero, 1)
            pool.affine_select(out=ident[:, :], in_=ident[:, :], compare_op=ALU.not_equal, fill=1.0, base=0,
                               pattern=[[-1, P]], channel_multiplier=1).then_inc(id_ready, 1)
            pool.memset(v_out[:, :, :, :, :], 1.0).then_inc(v_pad, 1)

            def body(r, first, last):
                for j in range(2):
                    for m in range(4):
                        n = 4 * (2 * r + j) + m
                        pool.wait_ge(mid_ready, n + 1)
                        pool.tensor_tensor(parts[:, m % 2, 2], rest[:, m % 2], parts[:, m % 2, 1], ALU.subtract) \
                            .then_inc(lo_ready, 1)
            peeled(pool, n_iter, body)

        @block.tensor
        def _(pe):
            pe.wait_ge(id_ready, 1)
            pe.wait_ge(w_loaded, 16 * 12)
            for i in range(3):
                for c in range(2):
                    n = 2 * i + c
                    if n >= 2:
                        pe.wait_ge(w_ready, n - 1)
                    for t in range(2):
                        mm = pe.transpose(tr_ps[:, n % 2, t * P:(t + 1) * P], w_in[:, i, t, c * P:(c + 1) * P], ident[:, :])
                    mm.then_inc(w_tr, 1)
            pe.wait_ge(w_ready, 6)

            def transposes(r, j):
                pe.wait_ge(x_loaded[j], 16 * (r + 1))
                for c in range(2):
                    for t in range(CT):
                        mm = pe.transpose(tr_ps[:, c, t * P:(t + 1) * P], x_in[:, j, t, c * P:(c + 1) * P], ident[:, :])
                    mm.then_inc(xt_mm, 1)

            transposes(0, 0)

            def body(r, first, last):
                for j in range(2):
                    pe.wait_ge(xt_ready, 2 * (2 * r + j) + 2)
                    for m in range(4):
                        n = 4 * (2 * r + j) + m
                        if m >= 2 or j or not first:
                            pe.wait_ge(full_ready, n - 1)
                        for c in range(2):
                            mm = pe.matmul(pr_ps[:, m % 2], w_t[:, m // 2, c, (m % 2) * P:(m % 2 + 1) * P],
                                           x_t[:, j, c], start=(c == 0), stop=(c == 1))
                        mm.then_inc(pr_mm, 1)
                    if j == 0 or not last:
                        transposes(r + j, 1 - j)
                    for h in range(2):
                        if j or not first:
                            pe.wait_ge(v_ready, 2 * (2 * r + j) + h - 1)
                        for t in range(2):
                            for c in range(2):
                                mm = pe.matmul(v_ps[:, h, t], x_t[:, j, c, (2 * h + t) * P:(2 * h + t + 1) * P],
                                               w_t[:, 2, c], start=(t == 0 and c == 0), stop=(c == 1),
                                               skip_group_check=True)
                        mm.then_inc(v_mm, 1)
            peeled(pe, n_iter, body)

        @block.scalar
        def _(act):
            for n in range(6):
                act.wait_ge(w_tr, n + 1)
                act.activation(w_t[:, n // 2, n % 2], tr_ps[:, n % 2, 0:dim], ACT.Copy).then_inc(w_ready, 1)

            def take_x(r, j):
                for c in range(2):
                    act.wait_ge(xt_mm, 2 * (2 * r + j) + c + 1)
                    act.activation(x_t[:, j, c], tr_ps[:, c], ACT.Copy).then_inc(xt_ready, 1)

            take_x(0, 0)

            def body(r, first, last):
                for j in range(2):
                    def middle(m):
                        act.wait_ge(rest_ready, 4 * (2 * r + j) + m + 1)
                        if m >= 2 or j or not first:
                            act.wait_ge(part_saved[m % 2], 16 * (2 * (2 * r + j) + m // 2))
                        act.activation(parts[:, m % 2, 1], rest[:, m % 2], ACT.Copy).then_inc(mid_ready, 1)

                    for m in range(4):
                        n = 4 * (2 * r + j) + m
                        act.wait_ge(pr_mm, n + 1)
                        if m >= 2 or j or not first:
                            act.wait_ge(rest_ready, n - 1)
                        if m < 2:
                            act.activation(full[:, m % 2], pr_ps[:, m % 2], ACT.Copy, scale=float(HD) ** -0.5) \
                                .then_inc(full_ready, 1)
                        else:
                            act.activation(full[:, m % 2], pr_ps[:, m % 2], ACT.Identity, bias=pe0[:, 0:1]) \
                                .then_inc(full_ready, 1)
                        if m:
                            middle(m - 1)
                    if j == 0 or not last:
                        if j or not first:
                            act.wait_ge(v_mm, 2 * (2 * r + j))
                        take_x(r + j, 1 - j)
                    middle(3)
            peeled(act, n_iter, body)

        @block.vector
        def _(dve):
            dve.wait_ge(w_loaded, 16 * 12)
            dve.wait_ge(v_pad, 1)

            def body(r, first, last):
                for j in range(2):
                    for m in range(4):
                        n = 4 * (2 * r + j) + m
                        dve.wait_ge(full_ready, n + 1)
                        if m >= 2 or j or not first:
                            dve.wait_ge(part_saved[m % 2], 16 * (2 * (2 * r + j) + m // 2))
                        dve.tensor_copy(parts[:, m % 2, 0], full[:, m % 2]).then_inc(hi_ready, 1)
                        dve.wait_ge(hi_ready, n + 1)
                        if m >= 2 or j or not first:
                            dve.wait_ge(lo_ready, n - 1)
                        dve.tensor_tensor(rest[:, m % 2], full[:, m % 2], parts[:, m % 2, 0], ALU.subtract) \
                            .then_inc(rest_ready, 1)
                    for h in range(2):
                        dve.wait_ge(v_mm, 2 * (2 * r + j) + h + 1)
                        if j or not first:
                            dve.wait_ge(v_saved[h], 16 * 4 * (2 * r + j))
                        dve.tensor_tensor(
                            v_out[:, h, :, :, 0:HD].rearrange("p t h c -> p (t h) c"),
                            v_ps[:, h].rearrange("p t (h c) -> p (t h) c", c=HD),
                            pv0[:, :].unsqueeze(1).to_broadcast([P, 2 * dim // HD, HD]), ALU.add).then_inc(v_ready, 1)
            peeled(dve, n_iter, body)


def attention(nc, qk_scr, v_scr, pek, pev, attn):
    n_iter, halves_, width, seq = attn.shape
    QB = seq // P
    TILES = 2 * QB
    RING = 3
    DEPTH = 4
    VW = 2 * HD
    assert QB == 8 and halves_ == 2 and width == GRP * VW and BAND == 3 * P
    with ExitStack() as ctx:
        sb = lambda n, s, d=F32: ctx.enter_context(nc.sbuf_tensor(n, s, d))
        ps = lambda n, s: ctx.enter_context(nc.psum_tensor(n, s, F32))
        sem = lambda n: ctx.enter_context(nc.semaphore(n))
        sem2 = lambda n: [sem(f"{n}{i}") for i in range(2)]
        bias_scr = nc.dram_tensor("bias_scr", (2, GRP, P * PW), F32).ap()
        prob_scr = nc.dram_tensor("prob_scr", (4, GRP, PPITCH), F32).ap()
        ident = sb("a_ident", [P, P])
        pk_in = sb("a_pk_in", [HD, MAXD + 1])
        pk_diff = sb("a_pk_diff", [HD, MAXD])
        pk_rest = sb("a_pk_rest", [HD, MAXD])
        pk_parts = sb("a_pk_parts", [HD, 3, MAXD], BF16)
        pk = sb("a_pk", [P, MAXD], BF16)
        pv_in = sb("a_pv_in", [P, 2, HD])
        pv_0 = sb("a_pv_0", [P, HD])
        pv = sb("a_pv", [P, 2, VW])
        edge = sb("a_edge", [P, 2, P])
        q_s = sb("a_q", [P, 2, GRP, seq], BF16)
        k_s = sb("a_k", [P, 2, GRP, seq], BF16)
        v_s = sb("a_v", [P, 2, QB, GRP, VW])
        b_out = sb("a_b_out", [P, 2, GRP, MAXD])
        bias = sb("a_bias", [P, 2, GRP, BAND])
        neg_s = sb("a_neg_s", [P, 2, BAND])
        far_neg = sb("a_far_neg", [P, GRP])
        band_neg = sb("a_band_neg", [P, GRP])
        neg_max = sb("a_neg_max", [P, GRP])
        prob = sb("a_prob", [P, 2, GRP, seq])
        p_t = sb("a_p_t", [P, 2, GRP, seq])
        band = sb("a_band", [P, 2, GRP, MAXD])
        band_t = sb("a_band_t", [P, 2, GRP, MAXD])
        o_t = sb("a_o_t", [P, 2, P])
        s_ps = ps("a_s_ps", [P, 2, seq])
        t_ps = ps("a_t_ps", [P, RING, 512])
        o_ps = ps("a_o_ps", [P, 512])
        id_zero, id_ready, set_ready = sem("a_id_zero"), sem("a_id_ready"), sem("a_set_ready")
        pe_loaded, pk_step, pk_placed, pv_ready = sem("a_pe_loaded"), sem("a_pk_step"), sem("a_pk_placed"), sem("a_pv_ready")
        edge_saved = sem("a_edge_saved")
        qk_loaded, v_loaded = sem2("a_qk_loaded"), sem2("a_v_loaded")
        b_mm, b_evac = sem("a_b_mm"), sem("a_b_evac")
        b_saved, b_loaded = sem2("a_b_saved"), sem2("a_b_loaded")
        qk_mm, part_max, max_ready, exp_ready = sem("a_qk_mm"), sem("a_part_max"), sem("a_max_ready"), sem("a_exp_ready")
        p_saved, p_loaded = sem2("a_p_saved"), sem2("a_p_loaded")
        t_mm, r_mm = sem("a_t_mm"), sem("a_r_mm")
        t_evac = {"act": sem("a_t_evac_act"), "dve": sem("a_t_evac_dve")}
        r_evac = sem2("a_r_evac")
        o_mm, o_evac = sem("a_o_mm"), sem("a_o_evac")
        stored = sem2("a_stored")
        block = ctx.enter_context(nc.Block())

        OE = 0
        BIAS_SLOTS, BAND_SLOTS = (0, 1), (0, 1)
        QKN = 1
        VALUE_SLOTS = (1, 2, 3)
        ORDER = [q for pair in zip(range(QB - 1, QB // 2 - 1, -1), range(QB // 2)) for q in pair]

        def q_block(k):
            return ORDER[k % QB]

        def band_start(qb):
            return BAND - min(qb + 1, 3) * P

        def halves(qb):
            h = P // 2
            return ((slice(0, h), slice(band_start(qb), BAND - h)), (slice(h, P), slice(max(band_start(qb), h), BAND)))

        def first_j(qb):
            return P if qb == 0 else 0

        def prob_slot(k):
            return 2 + q_block(k) if q_block(k) < 2 else k % 2

        def upto(per_tile, r, k):
            whole = sum(per_tile(q_block(t)) for t in range(TILES))
            return r * whole + (k // TILES) * whole + sum(per_tile(q_block(t)) for t in range(k % TILES))

        def t_banks(qb):
            return [range(b, min(b + 4, qb + 1)) for b in range(0, qb + 1, 4)]

        def t_engine(qb, u, i):
            return ("dve", "act")[i if qb >= 4 else u % 2]

        def band_engine(qb, i):
            return ("dve", "act")[i]

        def t_done(eng, r, k, u, i):
            banks = lambda qb: [(h, b) for h in range(GRP) for b in range(len(t_banks(qb))) if t_engine(qb, h, b) == eng]
            of_tile = banks(q_block(k))
            return upto(lambda qb: len(banks(qb)), r, k) + (len(of_tile) if i < 0 else of_tile.index((u, i)) + 1)

        def t_made(r, k, u):
            return upto(lambda qb: GRP * len(t_banks(qb)), r, k) + (u + 1) * len(t_banks(q_block(k)))

        def pair(r, k):
            return 16 * (QB * r + k // 2 + 1)

        def valid(kk, first, last):
            return (kk >= 0 or not first) and (kk < TILES or not last)

        def plan(k, first, last):
            jobs = []
            ok = lambda kk: valid(kk, first, last)
            for u in range(GRP):
                if ok(k + 2) and u in BIAS_SLOTS:
                    jobs.append(("bias", u, k + 2, BIAS_SLOTS.index(u)))
                if ok(k - 1):
                    jobs += [("p", u, k - 1, i) for i in range(len(t_banks(q_block(k - 1))))]
                if ok(k - 2) and u in BAND_SLOTS:
                    jobs.append(("band", u, k - 2, BAND_SLOTS.index(u)))
            return jobs

        def bank_user_before(k, pos, first, last):
            users = [job for job in [plan(k, first, last)[n] for n in range(pos % RING, pos, RING)]]
            back = 0
            while not users and back < 3:
                back += 1
                users = plan(k - back, first, last)[pos % RING::RING]
            return users[-1] if users else None

        def wait_evac(eng, r, job):
            kind, u, kk, i = job
            if kind == "band":
                eng.wait_ge(r_evac[i], TILES * r + kk + 1)
            elif kind == "p":
                who = t_engine(q_block(kk), u, i)
                eng.wait_ge(t_evac[who], t_done(who, r, kk, u, i))
            else:
                eng.wait_ge(b_evac, 2 * (TILES * r + kk) + i + 1)

        def steps(first, last):
            return range(-2 if first else 0, TILES + (DEPTH - 1 if last else 0))

        def ahead(k, u, last):
            k, u = k + (u + 1) // GRP, (u + 1) % GRP
            return (k, u) if k >= 0 and (k < TILES or not last) else None

        def read_out(eng, copy, name, r, k, u, first, last):
            for pos, (kind, uu, kk, i) in enumerate(plan(k, first, last)):
                if uu != u:
                    continue
                par, bank, j = kk % 2, t_ps[:, pos % RING], first_j(q_block(kk))
                by_head = bank.rearrange("p (h j) -> p h j", h=2)[:, :, j:]
                if kind == "p" and t_engine(q_block(kk), u, i) == name:
                    blocks = t_banks(q_block(kk))[i]
                    eng.wait_ge(t_mm, t_made(r, kk, u) - len(t_banks(q_block(kk))) + i + 1)
                    if valid(kk - 2, first, last):
                        eng.wait_ge(o_mm, TILES * r + kk - 1)
                    copy(p_t[:, par, u, blocks[0] * P:(blocks[-1] + 1) * P], bank[:, 0:len(blocks) * P]) \
                        .then_inc(t_evac[name], 1)
                if kind == "band" and band_engine(q_block(kk), i) == name:
                    eng.wait_ge(r_mm, 2 * (TILES * r + kk) + i + 1)
                    if valid(kk - 2, first, last):
                        eng.wait_ge(o_mm, TILES * r + kk - 1)
                    copy(band_t[:, par, 2 * i:2 * i + 2, j:], by_head).then_inc(r_evac[i], 1)
                if kind == "bias" and name == "act":
                    eng.wait_ge(b_mm, 2 * (TILES * r + kk) + i + 1)
                    if i == 0 and valid(kk - 2, first, last):
                        eng.wait_ge(b_saved[par], pair(r, kk - 2))
                    copy(b_out[:, par, 2 * i:2 * i + 2, j:], by_head).then_inc(b_evac, 1)

        @block.sync
        def _(sp):
            sp.dma_start(pk_in[:, :], pek[0:MAXD + 1, :].rearrange("j d -> d j"), allow_slow_non_contiguous=True).then_inc(pe_loaded, 16)
            sp.dma_start(pv_in[:, :, :], pev[1:MAXD + 1, :].rearrange("(b p) d -> p b d", p=P)).then_inc(pe_loaded, 16)
            sp.dma_start(pv_0[:, :], pev[0:1, :].to_broadcast([P, HD])).then_inc(pe_loaded, 16)

            def load_qk(r, g, some=slice(0, len(TERMS_Q))):
                rows = slice(g * GRP * HD, (g + 1) * GRP * HD)
                for dst, which, terms in ((q_s, 0, TERMS_Q), (k_s, 1, TERMS_K)):
                    for i, part in list(enumerate(terms))[some]:
                        sp.dma_start(dst[i * HD:(i + 1) * HD, g], qk_scr[which, r, part, rows, :]
                                     .rearrange("(h d) t -> d h t", d=HD)).then_inc(qk_loaded[g], 16)

            def load_v(r, g):
                sp.dma_start(v_s[:, g].rearrange("p b h c -> p b (h c)"),
                             v_scr[2 * r + g].rearrange("(b p) c -> p b c", p=P)).then_inc(v_loaded[g], 16)

            load_qk(0, 0)
            load_v(0, 0)
            sp.wait_ge(set_ready, 5)
            for slot in range(2):
                rows = bias_scr[slot].rearrange("h (q c) -> q h c", c=PW)
                for i, at in ((0, 0), (1, P + MAXD)):
                    sp.dma_start(rows[:, :, at:at + P], edge[:, i].unsqueeze(1).to_broadcast([P, GRP, P])) \
                        .then_inc(edge_saved, 16)
            sp.wait_ge(pk_step, 5)
            for i, part in enumerate(TERMS_K):
                sp.dma_start(pk[i * HD:(i + 1) * HD, :], pk_parts[:, part]).then_inc(pk_placed, 16)
            for slot in (2, 3):
                rows = prob_scr[slot][:, 0:P * BAND].rearrange("h (q c) -> q h c", c=BAND)
                for at in (0, P):
                    sp.dma_start(rows[:, :, at:at + P], edge[:, 0].unsqueeze(1).to_broadcast([P, GRP, P])) \
                        .then_inc(edge_saved, 16)
            sp.wait_ge(edge_saved, 16 * 8)

            def body(r, first, last):
                r_prev = r - 1 if first or last else sp.snap(r - 1)
                r_next = r + 1 if first or last else sp.snap(r + 1)
                for k in steps(first, last):
                    ok = lambda kk: valid(kk, first, last)
                    T = TILES * r + k
                    if k + 1 >= 0 and ok(k + 1):
                        par = (k + 1) % 2
                        sp.wait_ge(b_saved[par], pair(r, k + 1))
                        src = bias_scr[par][:, P - 1:P - 1 + P * (PW - 1)].rearrange("h (q c) -> q h c", c=PW - 1)
                        for q, c in halves(q_block(k + 1)):
                            sp.dma_start(bias[q, par, :, c], src[q, :, c]).then_inc(b_loaded[par], 16)
                    if k >= 0 and ok(k - 1) and k - 1 < TILES:
                        par = (k - 1) % 2
                        sp.wait_ge(p_saved[par], 2 * pair(r, k - 1))
                        src = prob_scr[prob_slot(k - 1)][:, 1:1 + P * (BAND + 1)] \
                            .rearrange("h (q c) -> q h c", c=BAND + 1)
                        j = first_j(q_block(k - 1))
                        sp.dma_start(band[:, par, :, j:MAXD], src[:, :, j:MAXD]).then_inc(p_loaded[par], 16)
                    g_next = k // QB + 1
                    if 0 <= k < TILES and (g_next == 1 or not last):
                        if k % QB == 0:
                            if ok(k - 1):
                                sp.wait_ge(qk_mm, 4 * TILES * r + 4 * k)
                        if k % QB < 6 // QKN:
                            load_qk(r_next if g_next == 2 else r, g_next % 2, slice(QKN * (k % QB), QKN * (k % QB + 1)))
                        if k % QB == 3:
                            if ok(k - 4):
                                sp.wait_ge(o_mm, T - 3)
                            load_v(r_next if g_next == 2 else r, g_next % 2)
                    if ok(k + 2):
                        par = k % 2
                        sp.wait_ge(b_evac, 2 * TILES * r + 2 * k + 6)
                        rows = bias_scr[par].rearrange("h (q c) -> q h c", c=PW)
                        j = first_j(q_block(k + 2))
                        sp.dma_start(rows[:, :, P + j:P + MAXD], b_out[:, par, :, j:MAXD]).then_inc(b_saved[par], 16)
                    if k >= 0 and ok(k - 3):
                        par = (k - 3) % 2
                        qb, g = q_block(k - 3), ((k - 3) % TILES) // QB
                        if not ok(k + 2):
                            sp.wait_ge(o_evac, T - 2)
                        row = attn[r_prev if k < 3 else r]
                        sp.dma_start(row[g, :, qb * P:(qb + 1) * P], o_t[:, par]).then_inc(stored[par], 16)
                    if 0 <= k < TILES:
                        par, qb = k % 2, q_block(k)
                        sp.wait_ge(exp_ready, 4 * TILES * r + 4 * k + 4)
                        rows = prob_scr[prob_slot(k)][:, 0:P * BAND].rearrange("h (q c) -> q h c", c=BAND)
                        at = (qb - 2) * P
                        for q, c in halves(qb):
                            sp.dma_start(rows[q, :, c], prob[q, par, :, at + c.start:at + c.stop]).then_inc(p_saved[par], 16)
            peeled(sp, n_iter, body)
            for par in range(2):
                sp.wait_ge(stored[par], 16 * QB * n_iter)
                sp.wait_ge(b_saved[par], 16 * QB * n_iter)
                sp.wait_ge(p_saved[par], 32 * QB * n_iter)

        @block.gpsimd
        def _(pool):
            fills = ((edge[:, 0], 0.0), (edge[:, 1], NEG), (pv[:, :, HD:VW], 0.0),
                     (bias[0:P // 2, :, :, BAND - P // 2:BAND], NEG),
                     (bias[P // 2:P, :, :, 0:P // 2], 0.0))
            for n, (tile, number) in enumerate(fills):
                if n:
                    pool.wait_ge(set_ready, n)
                pool.memset(tile, number).then_inc(set_ready, 1)
            pool.wait_ge(set_ready, len(fills))
            pool.memset(ident[:, :], 0.0).then_inc(id_zero, 1)
            pool.wait_ge(id_zero, 1)
            pool.affine_select(out=ident[:, :], in_=ident[:, :], compare_op=ALU.not_equal, fill=1.0, base=0,
                               pattern=[[-1, P]], channel_multiplier=1).then_inc(id_ready, 1)

        @block.tensor
        def _(pe):
            pe.wait_ge(id_ready, 1)
            pe.wait_ge(pk_placed, 16 * len(TERMS_K))
            pe.wait_ge(pv_ready, 1)

            def scores(r, k, u, first, last):
                g, qb = (k // QB) % 2, q_block(k)
                unit = 4 * (TILES * r + k) + u
                if not (first and 4 * k + u < 2):
                    pe.wait_ge(exp_ready, unit - 1)
                for c in range(0, (qb + 1) * P, 512):
                    e = min(c + 512, (qb + 1) * P)
                    mm = pe.matmul(s_ps[:, u % 2, c:e], q_s[0:ROWS, g, u, qb * P:(qb + 1) * P],
                                   k_s[0:ROWS, g, u, c:e], start=True, stop=True)
                mm.then_inc(qk_mm, 1)

            def biases(r, k, c, bank):
                g, qb = (k // QB) % 2, q_block(k)
                if k % QB == 0 and c == 0:
                    pe.wait_ge(qk_loaded[g], 16 * 12 * (r + k // TILES + 1))
                j = first_j(qb)
                for h in range(2):
                    mm = pe.matmul(bank[:, h * MAXD + j:(h + 1) * MAXD], q_s[0:ROWS, g, 2 * c + h, qb * P:(qb + 1) * P], pk[0:ROWS, j:],
                                   start=(h == 0), stop=True, skip_group_check=True)
                mm.then_inc(b_mm, 1)

            def values(r, k, part, first, last):
                g, qb, par = (k // QB) % 2, q_block(k), k % 2
                js = [j for j in range(qb + 3) if j <= qb or (j - qb - 1) * P >= first_j(qb)]
                cuts = [min(qb + 1, len(js) * n // len(VALUE_SLOTS)) for n in range(len(VALUE_SLOTS))] + [len(js)]
                if part == 0:
                    for name in ("act", "dve"):
                        pe.wait_ge(t_evac[name], t_done(name, r, k, 0, -1))
                    if k % QB == 0:
                        pe.wait_ge(v_loaded[g], 16 * (r + k // TILES + 1))
                    if valid(k - 1, first, last):
                        pe.wait_ge(o_evac, TILES * r + k)
                if part == len(VALUE_SLOTS) - 1:
                    for i in range(2):
                        pe.wait_ge(r_evac[i], TILES * r + k + 1)
                for j in js[cuts[part]:cuts[part + 1]]:
                    for h in range(GRP):
                        if j <= qb:
                            w, m = v_s[:, g, j, h], p_t[:, par, h, j * P:(j + 1) * P]
                        else:
                            w, m = pv[:, j - qb - 1], band_t[:, par, h, (j - qb - 1) * P:(j - qb) * P]
                        mm = pe.matmul(o_ps[h * VW:(h + 1) * VW, 0:P], w, m, start=(j == 0), stop=(j == qb + 2))
                if part == len(VALUE_SLOTS) - 1:
                    mm.then_inc(o_mm, 1)

            def body(r, first, last):
                for k in steps(first, last):
                    ok = lambda kk: valid(kk, first, last)
                    jobs = plan(k, first, last)
                    for u in range(GRP):
                        if ahead(k, u, last):
                            scores(r, *ahead(k, u, last), first, last)
                        if u in VALUE_SLOTS and ok(k - 2) and 0 <= k < TILES + 2:
                            values(r, k - 2, VALUE_SLOTS.index(u), first, last)
                        for pos, job in enumerate(jobs):
                            kind, uu, kk, i = job
                            if uu != u:
                                continue
                            bank = t_ps[:, pos % RING]
                            before = bank_user_before(k, pos, first, last)
                            if before:
                                wait_evac(pe, r, before)
                            if kind == "bias":
                                biases(r, kk, i, bank)
                            elif kind == "p":
                                pe.wait_ge(exp_ready, 4 * (TILES * r + kk) + u + 1)
                                for n, b in enumerate(t_banks(q_block(kk))[i]):
                                    mm = pe.transpose(bank[:, n * P:(n + 1) * P],
                                                      prob[:, kk % 2, u, b * P:(b + 1) * P], ident[:, :])
                                mm.then_inc(t_mm, 1)
                            else:
                                pe.wait_ge(p_loaded[kk % 2], pair(r, kk))
                                for n in range(4):
                                    if (n % 2) * P >= first_j(q_block(kk)):
                                        mm = pe.transpose(bank[:, n * P:(n + 1) * P],
                                                          band[:, kk % 2, 2 * i + n // 2, (n % 2) * P:(n % 2 + 1) * P],
                                                          ident[:, :])
                                mm.then_inc(r_mm, 1)
            peeled(pe, n_iter, body)

        @block.scalar
        def _(act):
            act.wait_ge(set_ready, 5)

            def body(r, first, last):
                for k in steps(first, last):
                    ok = lambda kk: valid(kk, first, last)
                    T = TILES * r + k
                    for u in range(GRP):
                        if 0 <= k < TILES:
                            par, qb = k % 2, q_block(k)
                            lo = max(0, qb - 2) * P
                            w = (qb + 1) * P - lo
                            if ok(k - 2):
                                act.wait_ge(t_mm, t_made(r, k - 2, u))
                                if u == 0:
                                    act.wait_ge(p_saved[par], 2 * pair(r, k - 2))
                            act.wait_ge(max_ready, 4 * T + u + 1)
                            e = act.activation(prob[:, par, u, lo:lo + w], neg_s[:, u % 2, 0:w], ACT.Exp,
                                               bias=neg_max[:, u:u + 1], scale=-1.0)
                            if lo:
                                e = act.activation(prob[:, par, u, 0:lo], s_ps[:, u % 2, 0:lo], ACT.Exp,
                                                   bias=neg_max[:, u:u + 1])
                            e.then_inc(exp_ready, 1)
                        if u == OE and ok(k - 3) and k >= 0:
                            act.wait_ge(o_mm, T - 2)
                            if ok(k - 5):
                                act.wait_ge(stored[(k - 3) % 2], pair(r, k - 5))
                            act.activation(o_t[:, (k - 3) % 2], o_ps[:, 0:P], ACT.Copy).then_inc(o_evac, 1)
                        read_out(act, lambda o, i: act.activation(o, i, ACT.Copy), "act", r, k, u, first, last)
            peeled(act, n_iter, body)

        @block.vector
        def _(dve):
            dve.wait_ge(pe_loaded, 16 * 3)
            dve.wait_ge(set_ready, 5)
            dve.tensor_scalar(pk_diff[:, :], pk_in[:, 1:MAXD + 1], pk_in[:, 0:1], None, ALU.subtract).then_inc(pk_step, 1)
            dve.tensor_tensor(pv[:, :, 0:HD], pv_in[:, :, :], pv_0[:, :].unsqueeze(1).to_broadcast([P, 2, HD]),
                              ALU.subtract).then_inc(pv_ready, 1)
            dve.wait_ge(pk_step, 1)
            dve.tensor_copy(pk_parts[:, 0], pk_diff[:, :]).then_inc(pk_step, 1)
            dve.wait_ge(pk_step, 2)
            dve.tensor_tensor(pk_rest[:, :], pk_diff[:, :], pk_parts[:, 0], ALU.subtract).then_inc(pk_step, 1)
            dve.wait_ge(pk_step, 3)
            dve.tensor_copy(pk_parts[:, 1], pk_rest[:, :]).then_inc(pk_step, 1)
            dve.wait_ge(pk_step, 4)
            dve.tensor_tensor(pk_parts[:, 2], pk_rest[:, :], pk_parts[:, 1], ALU.subtract).then_inc(pk_step, 1)

            def maximum(r, k, u):
                par, qb, T = k % 2, q_block(k), TILES * r + k
                lo = max(0, qb - 2) * P
                w = (qb + 1) * P - lo
                dve.wait_ge(qk_mm, 4 * T + u + 1)
                if u == 0:
                    dve.wait_ge(b_loaded[par], 2 * pair(r, k))
                if lo:
                    dve.tensor_reduce(far_neg[:, u:u + 1], s_ps[:, u % 2, 0:lo], AX.X, ALU.max,
                                      negate=True).then_inc(part_max, 1)
                else:
                    dve.memset(far_neg[:, u:u + 1], BIG).then_inc(part_max, 1)
                dve.tensor_tensor_reduce(neg_s[:, u % 2, 0:w], s_ps[:, u % 2, lo:lo + w],
                                         bias[:, par, u, BAND - w:BAND], -1.0, BIG, ALU.add, ALU.min,
                                         accum_out=band_neg[:, u:u + 1]).then_inc(part_max, 1)
                dve.wait_ge(part_max, 8 * T + 2 * u + 2)
                dve.tensor_tensor(neg_max[:, u:u + 1], far_neg[:, u:u + 1], band_neg[:, u:u + 1], ALU.min) \
                    .then_inc(max_ready, 1)

            def body(r, first, last):
                for k in steps(first, last):
                    ok = lambda kk: valid(kk, first, last)
                    T = TILES * r + k
                    for u in range(GRP):
                        if ahead(k, u, last):
                            maximum(r, *ahead(k, u, last))
                        read_out(dve, dve.tensor_copy, "dve", r, k, u, first, last)
            peeled(dve, n_iter, body)


def feed_forward(nc, x, attn, wo, wg, wu, wd, out):
    nb, seq, dim = x.shape
    hid = wg.shape[0]
    HC = hid // P
    assert dim == 2 * P and HC == 6 and seq == 2 * CHUNK
    x_d, o_d = (t.rearrange("b (c t p) d -> b c p t d", p=P, t=CT) for t in (x, out))
    a_d = attn.rearrange("r g p t -> r (g p) t").rearrange("r (h w d) t -> r w h d t", w=2, d=HD)
    with ExitStack() as ctx:
        sb = lambda n, s, d=F32: ctx.enter_context(nc.sbuf_tensor(n, s, d))
        ps = lambda n, s: ctx.enter_context(nc.psum_tensor(n, s, F32))
        sem = lambda n: ctx.enter_context(nc.semaphore(n))
        ident = sb("f_ident", [P, P])
        wo_in = sb("f_wo_in", [P, 2, dim])
        w_int = sb("f_w_int", [P, 2, HC, dim], I32)
        wd_int = sb("f_wd_int", [P, 2, hid], I32)
        wo_t = sb("f_wo_t", [P, 2, dim])
        w_t = sb("f_w_t", [P, 2, 2, hid])
        wd_t = sb("f_wd_t", [P, HC, dim])
        eps = sb("f_eps", [P, CT])
        neg_half = sb("f_neg_half", [P, CT])
        half = sb("f_half", [P, CT])
        inv_dim = sb("f_inv_dim", [P, CT])
        x_in = sb("f_x_in", [P, 2, CT, dim])
        a_in = sb("f_a_in", [P, 2, 2, 2, CHUNK])
        inverse = sb("f_inverse", [P, 2, CHUNK])
        a_t = sb("f_a_t", [P, 2, CHUNK])
        x1 = sb("f_x1", [P, CT, dim])
        z = sb("f_z", [P, 2, CT, dim])
        z_t = sb("f_z_t", [P, 2, CHUNK])
        gate = sb("f_gate", [P, 2, CHUNK])
        h_t = sb("f_h_t", [P, HC, CHUNK])
        x2 = sb("f_x2", [P, CT, dim])
        o_out = sb("f_o_out", [P, 2, CT, dim])
        stats = sb("f_stats", [P, 2, CT, 6])
        half_mean, half_diff, sq_sum = (sb(f"f_{n}", [P, 2, CT]) for n in ("half_mean", "half_diff", "sq_sum"))
        mean, diff, var_in, var_between, var, var_eps, rstd = (
            sb(f"f_{n}", [P, 2, CT]) for n in ("mean", "diff", "var_in", "var_between", "var", "var_eps", "rstd"))
        tr_ps = ps("f_tr_ps", [P, 2, CHUNK])
        y_ps = ps("f_y_ps", [P, 2, 2, dim])
        g_ps = ps("f_g_ps", [P, 2, CHUNK])
        u_ps = ps("f_u_ps", [P, 2, CHUNK])
        id_zero, id_ready, const_ready = sem("f_id_zero"), sem("f_id_ready"), sem("f_const_ready")
        w_loaded, w_cast, w_tr, w_ready = sem("f_w_loaded"), sem("f_w_cast"), sem("f_w_tr"), sem("f_w_ready")
        in_loaded = [sem(f"f_in_loaded{i}") for i in range(2)]
        inv_ready, at_ready = sem("f_inv_ready"), sem("f_at_ready")
        y_mm, y_taken = sem("f_y_mm"), sem("f_y_taken")
        d_mm, d_taken = sem("f_d_mm"), sem("f_d_taken")
        stat = [sem(f"f_stat{k}") for k in range(2)]
        ln_step = [sem(f"f_ln_step{k}") for k in range(2)]
        normed = [sem(f"f_normed{k}") for k in range(2)]
        zt_mm, zt_ready = sem("f_zt_mm"), sem("f_zt_ready")
        g_mm, g_ready, h_ready = sem("f_g_mm"), sem("f_g_ready"), sem("f_h_ready")
        stored = [sem(f"f_stored{i}") for i in range(2)]
        block = ctx.enter_context(nc.Block())
        LN_STEPS = 10

        def weight_jobs():
            for c in range(2):
                yield wo_t[:, c], [wo_in[:, t, c * P:(c + 1) * P] for t in range(2)]
            for i in range(2):
                for c in range(2):
                    for s in (0, 3):
                        yield (w_t[:, i, c, s * P:(s + 3) * P],
                               [w_int[:, i, t, c * P:(c + 1) * P].bitcast(F32) for t in range(s, s + 3)])
            for h in range(HC):
                yield wd_t[:, h], [wd_int[:, t, h * P:(h + 1) * P].bitcast(F32) for t in range(2)]

        @block.sync
        def _(sp):
            sp.dma_start(wo_in[:, :, :], wo.rearrange("(t p) d -> p t d", p=P)).then_inc(w_loaded, 16)
            for i, w in enumerate((wg, wu)):
                sp.dma_start(w_int[:, i], w.rearrange("(t p) d -> p t d", p=P)).then_inc(w_loaded, 16)
            sp.dma_start(wd_int[:, :, :], wd.rearrange("(t p) d -> p t d", p=P)).then_inc(w_loaded, 16)

            def load(r, j):
                sp.dma_start(x_in[:, j], x_d[r, j]).then_inc(in_loaded[j], 16)
                for k in range(2):
                    for w in range(2):
                        sp.dma_start(a_in[:, j, k, w], a_d[2 * r + k, w, :, :, j * CHUNK:(j + 1) * CHUNK]) \
                            .then_inc(in_loaded[j], 16)

            load(0, 0)
            load(0, 1)

            def body(r, first, last):
                for j in range(2):
                    c = 2 * r + j
                    if not last:
                        sp.wait_ge(y_taken, 2 * c + 2)
                        load(r + 1, j)
                    sp.wait_ge(normed[1], 4 * c + 4)
                    sp.dma_start(o_d[r, j], o_out[:, j]).then_inc(stored[j], 16)
            peeled(sp, nb, body)
            for j in range(2):
                sp.wait_ge(stored[j], 16 * nb)

        @block.gpsimd
        def _(pool):
            pool.memset(ident[:, :], 0.0).then_inc(id_zero, 1)
            pool.wait_ge(id_zero, 1)
            pool.affine_select(out=ident[:, :], in_=ident[:, :], compare_op=ALU.not_equal, fill=1.0, base=0,
                               pattern=[[-1, P]], channel_multiplier=1).then_inc(id_ready, 1)
            pool.memset(eps[:, :], EPS).then_inc(const_ready, 1)
            pool.memset(neg_half[:, :], -0.5).then_inc(const_ready, 1)
            pool.memset(half[:, :], 0.5).then_inc(const_ready, 1)
            pool.memset(inv_dim[:, :], 1.0 / dim).then_inc(const_ready, 1)
            pool.wait_ge(const_ready, 4)

            def moments(c, k):
                pool.wait_ge(stat[k], 4 * c + 4)
                base = LN_STEPS * c
                s = stats[:, k]
                inc = lambda ins: ins.then_inc(ln_step[k], 1)
                inc(pool.tensor_tensor(half_mean[:, k], s[:, :, 1], s[:, :, 4], ALU.add))
                inc(pool.tensor_tensor(half_diff[:, k], s[:, :, 1], s[:, :, 4], ALU.subtract))
                inc(pool.tensor_tensor(sq_sum[:, k], s[:, :, 2], s[:, :, 5], ALU.add))
                pool.wait_ge(ln_step[k], base + 3)
                inc(pool.tensor_tensor(mean[:, k], half_mean[:, k], half[:, :], ALU.mult))
                inc(pool.tensor_tensor(diff[:, k], half_diff[:, k], half[:, :], ALU.mult))
                inc(pool.tensor_tensor(var_in[:, k], sq_sum[:, k], inv_dim[:, :], ALU.mult))
                pool.wait_ge(ln_step[k], base + 6)
                inc(pool.tensor_tensor(var_between[:, k], diff[:, k], diff[:, k], ALU.mult))
                pool.wait_ge(ln_step[k], base + 7)
                inc(pool.tensor_tensor(var[:, k], var_in[:, k], var_between[:, k], ALU.add))
                pool.wait_ge(ln_step[k], base + 8)
                inc(pool.tensor_tensor(var_eps[:, k], var[:, k], eps[:, :], ALU.add))
                pool.wait_ge(ln_step[k], base + 9)
                inc(pool.tensor_tensor(rstd[:, k], var_eps[:, k], neg_half[:, :], ALU.pow))

            moments(0, 0)

            def body(r, first, last):
                for j in range(2):
                    if j == 0 or not last:
                        moments(2 * r + j + 1, 0)
                    moments(2 * r + j, 1)
            peeled(pool, nb, body)

        @block.tensor
        def _(pe):
            pe.wait_ge(id_ready, 1)
            pe.wait_ge(w_loaded, 16 * 4)
            pe.wait_ge(w_cast, 3)
            for n, (_, pieces) in enumerate(weight_jobs()):
                if n >= 2:
                    pe.wait_ge(w_ready, n - 1)
                for t, piece in enumerate(pieces):
                    mm = pe.transpose(tr_ps[:, n % 2, t * P:(t + 1) * P], piece, ident[:, :])
                mm.then_inc(w_tr, 1)
            pe.wait_ge(w_ready, n + 1)

            def attn_output(c):
                pe.wait_ge(at_ready, 2 * c + 2)
                for b in range(2):
                    for t in range(2):
                        for k in range(2):
                            mm = pe.matmul(y_ps[:, b, t], a_t[:, k, (2 * b + t) * P:(2 * b + t + 1) * P], wo_t[:, k],
                                           start=(t == 0 and k == 0), stop=(k == 1), skip_group_check=True)
                    mm.then_inc(y_mm, 1)

            def z_transposes(j, c):
                for t in range(CT):
                    pe.wait_ge(normed[0], 4 * c + t + 1)
                    for k in range(2):
                        mm = pe.transpose(tr_ps[:, k, t * P:(t + 1) * P], z[:, j, t, k * P:(k + 1) * P], ident[:, :])
                        if t == CT - 1:
                            mm.then_inc(zt_mm, 1)

            attn_output(0)
            z_transposes(0, 0)

            def body(r, first, last):
                for j in range(2):
                    c = 2 * r + j
                    more = j == 0 or not last

                    def hidden(m):
                        n = HC * c + m
                        if m >= 2 or j or not first:
                            pe.wait_ge(h_ready, n - 1)
                        for ps_, i in ((g_ps, 0), (u_ps, 1)):
                            for k in range(2):
                                mm = pe.matmul(ps_[:, m % 2], w_t[:, i, k, m * P:(m + 1) * P], z_t[:, k],
                                               start=(k == 0), stop=(k == 1))
                        mm.then_inc(g_mm, 1)

                    pe.wait_ge(zt_ready, 2 * c + 2)
                    for m in range(3):
                        hidden(m)
                    hidden(3)
                    if more:
                        if j or not first:
                            pe.wait_ge(d_taken, 2 * c)
                        attn_output(c + 1)
                    hidden(4)
                    hidden(5)
                    if more:
                        pe.wait_ge(y_taken, 2 * c + 4)
                    for m in range(HC):
                        for b in range(2):
                            for t in range(2):
                                if b == 0 and t == 0:
                                    pe.wait_ge(h_ready, HC * c + m + 1)
                                mm = pe.matmul(y_ps[:, b, t], h_t[:, m, (2 * b + t) * P:(2 * b + t + 1) * P],
                                               wd_t[:, m], start=(m == 0 and t == 0), stop=(m == HC - 1),
                                               skip_group_check=True)
                            if m == HC - 1:
                                mm.then_inc(d_mm, 1)
                    if more:
                        z_transposes(1 - j, c + 1)
            peeled(pe, nb, body)

        @block.scalar
        def _(act):
            for n, (dst, pieces) in enumerate(weight_jobs()):
                act.wait_ge(w_tr, n + 1)
                act.activation(dst, tr_ps[:, n % 2, 0:P * len(pieces)], ACT.Copy).then_inc(w_ready, 1)

            def take(mm, ready, dst, c):
                for k in range(2):
                    act.wait_ge(mm, 2 * c + k + 1)
                    act.activation(dst[:, k], tr_ps[:, k], ACT.Copy).then_inc(ready, 1)

            take(zt_mm, zt_ready, z_t, 0)

            def body(r, first, last):
                for j in range(2):
                    c = 2 * r + j
                    for m in range(HC):
                        n = HC * c + m
                        act.wait_ge(g_mm, n + 1)
                        if m >= 2 or j or not first:
                            act.wait_ge(h_ready, n - 1)
                        act.activation(gate[:, m % 2], g_ps[:, m % 2], ACT.Silu).then_inc(g_ready, 1)
                    if j == 0 or not last:
                        take(zt_mm, zt_ready, z_t, c + 1)
            peeled(act, nb, body)

        @block.vector
        def _(dve):
            dve.wait_ge(w_loaded, 16 * 4)
            for src in (w_int[:, 0], w_int[:, 1], wd_int):
                src = src[:, :, :]
                dve.tensor_scalar(src.bitcast(F32), src, W_SCALE, None, ALU.mult).then_inc(w_cast, 1)

            def residual(mm, taken, dst, other, c):
                for b in range(2):
                    dve.wait_ge(mm, 2 * c + b + 1)
                    dve.tensor_tensor(dst[:, 2 * b:2 * b + 2], other[:, 2 * b:2 * b + 2], y_ps[:, b], ALU.add) \
                        .then_inc(taken, 1)

            def norm(k, c, src, taken, dst):
                dve.wait_ge(taken, 2 * c + 2)
                for t in range(CT):
                    dve.bn_stats(stats[:, k, t], src[:, t]).then_inc(stat[k], 1)
                dve.wait_ge(ln_step[k], LN_STEPS * c + LN_STEPS)
                for t in range(CT):
                    dve.tensor_scalar(dst[:, t], src[:, t], mean[:, k, t:t + 1], rstd[:, k, t:t + 1],
                                      ALU.subtract, ALU.mult).then_inc(normed[k], 1)

            def normalise(chunk, j, loads):
                dve.wait_ge(in_loaded[j], 16 * 5 * loads)
                dve.reciprocal(inverse[:, :, :], a_in[:, j, :, 1]).then_inc(inv_ready, 1)
                dve.wait_ge(inv_ready, chunk + 1)
                for k in range(2):
                    dve.tensor_tensor(a_t[:, k], a_in[:, j, k, 0], inverse[:, k], ALU.mult).then_inc(at_ready, 1)

            normalise(0, 0, 1)
            residual(y_mm, y_taken, x1, x_in[:, 0], 0)
            norm(0, 0, x1, y_taken, z[:, 0])

            def body(r, first, last):
                for j in range(2):
                    c = 2 * r + j
                    more = j == 0 or not last
                    for m in range(HC):
                        n = HC * c + m
                        if m == 2 and more:
                            normalise(c + 1, 1 - j, r + j + 1)
                        if m == HC - 1 and more:
                            residual(y_mm, y_taken, x1, x_in[:, 1 - j], c + 1)
                        dve.wait_ge(g_ready, n + 1)
                        dve.tensor_tensor(h_t[:, m], gate[:, m % 2], u_ps[:, m % 2], ALU.mult).then_inc(h_ready, 1)
                    if more:
                        norm(0, c + 1, x1, y_taken, z[:, 1 - j])
                    residual(d_mm, d_taken, x2, z[:, j], c)
                    if not first:
                        dve.wait_ge(stored[j], 16 * r)
                    norm(1, c, x2, d_taken, o_out[:, j])
            peeled(dve, nb, body)


def build(nc, x, wq, wk, wv, wo, pek, pev, wg, wu, wd, out):
    nb, seq, dim = x.shape
    qk_scr = nc.dram_tensor("qk_scr", (2, nb * 2, 3, P, seq), BF16).ap()
    v_scr = nc.dram_tensor("v_scr", (nb * 4, seq, GRP * 2 * HD), F32).ap()
    attn = nc.dram_tensor("attn_scr", (nb * 2, 2, P, seq), F32).ap()
    project(nc, x, wq, wk, wv, pek, pev, qk_scr, v_scr)
    attention(nc, qk_scr, v_scr, pek, pev, attn)
    feed_forward(nc, x, attn, wo, wg, wu, wd, out)


_INS = ["L0_attn_x", "L0_attn_Wq", "L0_attn_Wk", "L0_attn_Wv", "L0_attn_Wo", "L0_attn_pek", "L0_attn_pev",
        "L0_ffn_w_gate", "L0_ffn_w_up", "L0_ffn_w_down"]


def kernel(**inputs):
    import numpy as _np
    import concourse.bacc as _bacc
    from concourse import mybir as _mybir
    from concourse.bass_utils import run_bass_kernel_spmd as _run

    nc = _bacc.Bacc("TRN2", target_bir_lowering=False, num_devices=1)
    arrays, args = {}, []
    for name in _INS:
        a = _np.ascontiguousarray(inputs[name])
        arrays[f"in_{name}"] = a
        args.append(nc.dram_tensor(f"in_{name}", a.shape, _mybir.dt.from_np(a.dtype), kind="ExternalInput").ap())
    out = nc.dram_tensor("out_0", inputs["L0_attn_x"].shape, _mybir.dt.float32, kind="ExternalOutput").ap()
    build(nc, *args, out)
    r = _run(nc, [arrays], core_ids=[0])
    return r.results[0]["out_0"]
```
